# Optimizing a Trainium2 kernel written in Bass

```python
import numpy as np
import jax
import jax.numpy as jnp

def _softmax(x, axis=-1):
    return jax.nn.softmax(x, axis=axis)

def _gelu(x):
    return jax.nn.gelu(x, approximate=True)

def _silu(x):
    return jax.nn.silu(x)

def _sigmoid(x):
    return jax.nn.sigmoid(x)

def _layernorm(x, axis=-1, eps=1e-05):
    m = jnp.mean(x, axis=axis, keepdims=True)
    v = jnp.var(x, axis=axis, keepdims=True)
    return (x - m) / jnp.sqrt(v + eps)

def _scatter_add(tgt, idx, src, axis=0):
    return tgt.at[idx].add(src)

def _segment_sum(src, seg, n):
    return jax.ops.segment_sum(src, seg, n)
kernel_name = 'mk_perceiver_d1_seqx_r4_b4b042'

def setup_inputs(seed: int=0):
    np.random.seed(seed)
    _w = jnp.asarray

    def _rec_inputs():
        import jax
        import jax.numpy as jnp
        _rk = jax.random.key(seed)
        x = 7.22e-05 + 1 * jax.random.normal(jax.random.fold_in(_rk, 1), (4, 256, 256), jnp.float32)
        _lenS = 256 - jax.random.randint(jax.random.fold_in(_rk, 7), (4,), 0, max(1, 256 // 4) + 1, jnp.int32)
        _lenS2 = 4096 - jax.random.randint(jax.random.fold_in(_rk, 8), (4,), 0, max(1, 4096 // 4) + 1, jnp.int32)
        _ctx_768P = jax.random.normal(jax.random.fold_in(_rk, 11), (4, 16, 192), jnp.float32)
        _ctx_768c = jax.random.dirichlet(jax.random.fold_in(_rk, 511), 0.3 * jnp.ones((16,), jnp.float32), (4, 4096))
        _ctx_768t = jnp.einsum('bsk,bkd->bsd', _ctx_768c, _ctx_768P)
        _ctx_768t = _ctx_768t * jax.lax.rsqrt(jnp.mean(jnp.square(_ctx_768t)) + 1e-12) * 0.953939
        ctx_768 = -0.000191848 + 0.999787 * (_ctx_768t + 0.3 * jax.random.normal(jax.random.fold_in(_rk, 611), (4, 4096, 192), jnp.float32))
        return (x, ctx_768)
    x, ctx_768 = _rec_inputs()

    def _L0_xattn_setup():
        import jax, jax.numpy as jnp
        import numpy as np
        NUM_HEADS = 16
        CLAMP = 10000.0
        key = jax.random.key(seed)
        ks = jax.random.split(key, 8)
        B, Nq, Nkv, Cq, Ckv = (4, 512, 512, 256, 192)
        s_q = 1.0 / np.sqrt(Cq)
        s_kv = 1.0 / np.sqrt(Ckv)
        return {'query': jax.random.normal(ks[0], (B, Nq, Cq), jnp.float32), 'key_value': jax.random.normal(ks[1], (B, Nkv, Ckv), jnp.float32), 'Wq': jax.random.normal(ks[2], (Cq, Cq), jnp.float32) * s_q, 'bq': jnp.zeros((Cq,), jnp.float32), 'Wk': jax.random.normal(ks[3], (Ckv, Cq), jnp.float32) * s_kv, 'bk': jnp.zeros((Cq,), jnp.float32), 'Wv': jax.random.normal(ks[4], (Ckv, Cq), jnp.float32) * s_kv, 'bv': jnp.zeros((Cq,), jnp.float32), 'Wo': jax.random.normal(ks[5], (Cq, Cq), jnp.float32) * s_q, 'bo': jnp.zeros((Cq,), jnp.float32)}
    _L0_xattn_all = _L0_xattn_setup()
    _L0_xattn_in = {k: v for k, v in _L0_xattn_all.items() if k in ('Wq', 'bq', 'Wk', 'bk', 'Wv', 'bv', 'Wo', 'bo')}
    del _L0_xattn_all

    def _L0_attn_setup():
        import math
        import jax, jax.numpy as jnp
        import numpy as np
        D_MODEL = 256
        N_HEADS = 16
        HEAD_DIM = D_MODEL // N_HEADS
        ROPE_THETA = 10000.0

        def _apply_rope(t, offset=0):
            B, H, T, Dh = t.shape
            inv_freq = 1.0 / ROPE_THETA ** (jnp.arange(0, Dh, 2, dtype=jnp.float32) / Dh)
            pos = jnp.arange(T, dtype=jnp.float32) + offset
            ang = pos[:, None] * inv_freq[None, :]
            cos = jnp.concatenate([jnp.cos(ang), jnp.cos(ang)], axis=-1)
            sin = jnp.concatenate([jnp.sin(ang), jnp.sin(ang)], axis=-1)
            t1, t2 = (t[..., :Dh // 2], t[..., Dh // 2:])
            rot = jnp.concatenate([-t2, t1], axis=-1)
            return t * cos + rot * sin

        def _forward(x, Wq, Wk, Wv, Wo):
            B, T, _ = x.shape
            scale = 1.0 / math.sqrt(HEAD_DIM)

            def split_heads(y):
                return y.reshape(B, T, N_HEADS, HEAD_DIM).transpose(0, 2, 1, 3)
            q = split_heads(x @ Wq.T)
            k = split_heads(x @ Wk.T)
            v = split_heads(x @ Wv.T)
            q = _apply_rope(q)
            k = _apply_rope(k)
            scores = jnp.einsum('bhtd,bhsd->bhts', q, k) * scale
            causal = jnp.triu(jnp.ones((T, T), dtype=bool), k=1)
            scores = jnp.where(causal[None, None], -jnp.inf, scores)
            attn = jax.nn.softmax(scores, axis=-1)
            attn = jnp.nan_to_num(attn, nan=0.0)
            out = jnp.einsum('bhts,bhsd->bhtd', attn, v)
            out = out.transpose(0, 2, 1, 3).reshape(B, T, N_HEADS * HEAD_DIM)
            return out @ Wo.T
        key = jax.random.key(seed)
        ks = jax.random.split(key, 5)
        B, T = (4, 512)
        w_scale = math.sqrt(2.0 / (D_MODEL + D_MODEL))
        return {'x': jax.random.normal(ks[0], (B, T, D_MODEL), dtype=jnp.float32), 'Wq': jax.random.normal(ks[1], (D_MODEL, D_MODEL), dtype=jnp.float32) * w_scale, 'Wk': jax.random.normal(ks[2], (D_MODEL, D_MODEL), dtype=jnp.float32) * w_scale, 'Wv': jax.random.normal(ks[3], (D_MODEL, D_MODEL), dtype=jnp.float32) * w_scale, 'Wo': jax.random.normal(ks[4], (D_MODEL, D_MODEL), dtype=jnp.float32) * w_scale}
    _L0_attn_all = _L0_attn_setup()
    _L0_attn_in = {k: v for k, v in _L0_attn_all.items() if k in ('Wq', 'Wk', 'Wv', 'Wo')}
    del _L0_attn_all

    def _L0_ffn_setup():
        import jax, jax.numpy as jnp
        import numpy as np
        from jax import lax
        D = 256
        H = 1024
        E = 8
        TOPK = 2
        key = jax.random.key(seed)
        ks = jax.random.split(key, 7)
        s = 0.02
        return {'x': jax.random.normal(ks[0], (2, 512, D), dtype=jnp.float32), 'W1': jax.random.normal(ks[1], (E, D, H), dtype=jnp.float32) * s, 'b1': jnp.zeros((E, H), dtype=jnp.float32), 'W2': jax.random.normal(ks[2], (E, H, D), dtype=jnp.float32) * s, 'b2': jnp.zeros((E, D), dtype=jnp.float32), 'Wr': jax.random.normal(ks[3], (D, E), dtype=jnp.float32) * s, 'br': jnp.zeros((E,), dtype=jnp.float32)}
    _L0_ffn_all = _L0_ffn_setup()
    _L0_ffn_in = {k: v for k, v in _L0_ffn_all.items() if k in ('W1', 'b1', 'W2', 'b2', 'Wr', 'br')}
    del _L0_ffn_all
    return {'x': x, 'ctx_768': ctx_768, 'L0_xattn_Wq': _L0_xattn_in['Wq'], 'L0_xattn_bq': _L0_xattn_in['bq'], 'L0_xattn_Wk': _L0_xattn_in['Wk'], 'L0_xattn_bk': _L0_xattn_in['bk'], 'L0_xattn_Wv': _L0_xattn_in['Wv'], 'L0_xattn_bv': _L0_xattn_in['bv'], 'L0_xattn_Wo': _L0_xattn_in['Wo'], 'L0_xattn_bo': _L0_xattn_in['bo'], 'L0_attn_Wq': _L0_attn_in['Wq'], 'L0_attn_Wk': _L0_attn_in['Wk'], 'L0_attn_Wv': _L0_attn_in['Wv'], 'L0_attn_Wo': _L0_attn_in['Wo'], 'L0_ffn_W1': _L0_ffn_in['W1'], 'L0_ffn_b1': _L0_ffn_in['b1'], 'L0_ffn_W2': _L0_ffn_in['W2'], 'L0_ffn_b2': _L0_ffn_in['b2'], 'L0_ffn_Wr': _L0_ffn_in['Wr'], 'L0_ffn_br': _L0_ffn_in['br']}

def reference(x, ctx_768, L0_xattn_Wq, L0_xattn_bq, L0_xattn_Wk, L0_xattn_bk, L0_xattn_Wv, L0_xattn_bv, L0_xattn_Wo, L0_xattn_bo, L0_attn_Wq, L0_attn_Wk, L0_attn_Wv, L0_attn_Wo, L0_ffn_W1, L0_ffn_b1, L0_ffn_W2, L0_ffn_b2, L0_ffn_Wr, L0_ffn_br):
    import jax
    import jax.numpy as jnp

    def _L0_xattn_ref(query, key_value, Wq, bq, Wk, bk, Wv, bv, Wo, bo):
        import jax, jax.numpy as jnp
        import numpy as np
        NUM_HEADS = 16
        CLAMP = 10000.0
        B, Nq, Cq = query.shape
        Nkv = key_value.shape[1]
        H = NUM_HEADS
        D = Cq // H
        scale = D ** (-0.5)
        q = (query @ Wq + bq).reshape(B, Nq, H, D).transpose(0, 2, 1, 3)
        k = (key_value @ Wk + bk).reshape(B, Nkv, H, D).transpose(0, 2, 1, 3)
        v = (key_value @ Wv + bv).reshape(B, Nkv, H, D).transpose(0, 2, 1, 3)
        attn = jnp.einsum('bhqd,bhkd->bhqk', q, k) * scale
        attn = jnp.clip(attn, -CLAMP, CLAMP)
        attn = jax.nn.softmax(attn, axis=-1)
        attn = jnp.where(jnp.any(jnp.isnan(attn)), jnp.asarray(1.0 / Nkv, attn.dtype), attn)
        x = jnp.einsum('bhqk,bhkd->bqhd', attn, v).reshape(B, Nq, Cq)
        return x @ Wo + bo

    def _L0_attn_ref(x, Wq, Wk, Wv, Wo):
        import math
        import jax, jax.numpy as jnp
        import numpy as np
        D_MODEL = 256
        N_HEADS = 16
        HEAD_DIM = D_MODEL // N_HEADS
        ROPE_THETA = 10000.0

        def _apply_rope(t, offset=0):
            B, H, T, Dh = t.shape
            inv_freq = 1.0 / ROPE_THETA ** (jnp.arange(0, Dh, 2, dtype=jnp.float32) / Dh)
            pos = jnp.arange(T, dtype=jnp.float32) + offset
            ang = pos[:, None] * inv_freq[None, :]
            cos = jnp.concatenate([jnp.cos(ang), jnp.cos(ang)], axis=-1)
            sin = jnp.concatenate([jnp.sin(ang), jnp.sin(ang)], axis=-1)
            t1, t2 = (t[..., :Dh // 2], t[..., Dh // 2:])
            rot = jnp.concatenate([-t2, t1], axis=-1)
            return t * cos + rot * sin

        def _forward(x, Wq, Wk, Wv, Wo):
            B, T, _ = x.shape
            scale = 1.0 / math.sqrt(HEAD_DIM)

            def split_heads(y):
                return y.reshape(B, T, N_HEADS, HEAD_DIM).transpose(0, 2, 1, 3)
            q = split_heads(x @ Wq.T)
            k = split_heads(x @ Wk.T)
            v = split_heads(x @ Wv.T)
            q = _apply_rope(q)
            k = _apply_rope(k)
            scores = jnp.einsum('bhtd,bhsd->bhts', q, k) * scale
            causal = jnp.triu(jnp.ones((T, T), dtype=bool), k=1)
            scores = jnp.where(causal[None, None], -jnp.inf, scores)
            attn = jax.nn.softmax(scores, axis=-1)
            attn = jnp.nan_to_num(attn, nan=0.0)
            out = jnp.einsum('bhts,bhsd->bhtd', attn, v)
            out = out.transpose(0, 2, 1, 3).reshape(B, T, N_HEADS * HEAD_DIM)
            return out @ Wo.T
        return _forward(x, Wq, Wk, Wv, Wo)

    def _L0_ffn_ref(x, W1, b1, W2, b2, Wr, br):
        import jax, jax.numpy as jnp
        import numpy as np
        from jax import lax
        D = 256
        H = 1024
        E = 8
        TOPK = 2
        B, S, _ = x.shape
        xf = x.reshape(-1, D)
        logits = xf @ Wr + br
        topv, _ = lax.top_k(logits, TOPK)
        thresh = topv[:, TOPK - 1:TOPK]
        masked = jnp.where(logits >= thresh, logits, -jnp.inf)
        weights = jax.nn.softmax(masked, axis=-1)
        h = jax.nn.gelu(jnp.einsum('td,edh->eth', xf, W1) + b1[:, None, :], approximate=False)
        expert_out = jnp.einsum('eth,ehd->etd', h, W2) + b2[:, None, :]
        out = jnp.einsum('etd,te->td', expert_out, weights)
        return out.reshape(B, S, D)
    x = x + _L0_xattn_ref(_layernorm(x, axis=-1), ctx_768, L0_xattn_Wq, L0_xattn_bq, L0_xattn_Wk, L0_xattn_bk, L0_xattn_Wv, L0_xattn_bv, L0_xattn_Wo, L0_xattn_bo)
    x = x + _L0_attn_ref(_layernorm(x, axis=-1), L0_attn_Wq, L0_attn_Wk, L0_attn_Wv, L0_attn_Wo)
    x = x + _L0_ffn_ref(_layernorm(x, axis=-1), L0_ffn_W1, L0_ffn_b1, L0_ffn_W2, L0_ffn_b2, L0_ffn_Wr, L0_ffn_br)
    return x

_drawn_inputs = setup_inputs


def setup_inputs(seed=0):
    import zlib

    import numpy as np

    out = dict(_drawn_inputs(seed))
    spreads = {'L0_xattn_bq': (0.0, 0.296),
     'L0_xattn_bk': (0.0, 0.8),
     'L0_xattn_bv': (0.0, 0.1),
     'L0_xattn_bo': (0.0, 0.1),
     'L0_ffn_b1': (0.0, 0.377),
     'L0_ffn_b2': (0.0, 0.1),
     'L0_ffn_br': (0.0, 0.1)}
    factors = {}
    for name, (base, spread) in spreads.items():
        noise = np.random.default_rng([zlib.crc32(name.encode()), seed]).standard_normal(out[name].shape)
        drawn = base * np.exp(spread * noise) if base else spread * noise
        out[name] = jnp.asarray(drawn.astype(out[name].dtype))
    for name, factor in factors.items():
        out[name] = (out[name] * factor).astype(out[name].dtype)
    return out
```

```python
from contextlib import ExitStack

import numpy as np

import concourse.bass as bass
from concourse import mybir

F32 = mybir.dt.float32
BF16 = mybir.dt.bfloat16
ALU = mybir.AluOpType
ACT = mybir.ActivationFunctionType
AX = mybir.AxisListType

P = 128
B, T, D = 4, 256, 256
S, DC = 4096, 192
H = 16
DH = D // H
NH = B * H
TOK = B * T
NT = TOK // P
FC = D // P
E, HID = 8, 1024
HC = HID // P
KB = 512
NBLK = B * S // KB
NC = S // P
VW = DH + 1
PARTS = 6 * DH
K_PART = (0, 0, 0, 1, 1, 2)
Q_PART = (0, 1, 2, 0, 1, 0)
SCALE = DH ** -0.5
CLAMP = 10000.0
EPS = 1e-5
LOW = 64.0
FLOOR = float(np.exp(-LOW))


def layer_norm_steps(dve, nc, sem, base, x, stats, mv, ve, first=None):
    for t in range(NT):
        last = dve.bn_stats(stats[:, t, :], x[:, t, :])
    last.then_inc(sem, 1)
    dve.wait_ge(sem, base + 1)
    for t in range(NT):
        last = dve.bn_aggr(mv[:, t, :], stats[:, t, :])
    last.then_inc(sem, 1)
    dve.wait_ge(sem, base + 2)
    dve.tensor_scalar(ve[:], mv[:, :, 1], EPS, None, ALU.add).then_inc(sem, 1)


def build_program(nc, a, out):
    with ExitStack() as life:
        def dram(name, shape, dt):
            return nc.dram_tensor(name, shape, dt).ap()

        def sem(name):
            return life.enter_context(nc.semaphore(name))

        psum = life.enter_context(nc.psum_tensor("psum", [P, 8, 512], F32))
        x_sb = life.enter_context(nc.sbuf_tensor("x_sb", [P, NT, D], F32))
        ident = life.enter_context(nc.sbuf_tensor("ident", [P, P], F32))
        identb = life.enter_context(nc.sbuf_tensor("identb", [P, P], BF16))
        ones_row = life.enter_context(nc.sbuf_tensor("ones_row", [1, P], F32))
        neg_half = life.enter_context(nc.sbuf_tensor("neg_half", [P, NT], F32))
        stats = life.enter_context(nc.sbuf_tensor("stats", [P, NT, 6], F32))
        mv = life.enter_context(nc.sbuf_tensor("mv", [P, NT, 2], F32))
        ve = life.enter_context(nc.sbuf_tensor("ve", [P, NT], F32))
        rstd = life.enter_context(nc.sbuf_tensor("rstd", [P, NT], F32))
        o_all = life.enter_context(nc.sbuf_tensor("o_all", [P, FC, NH * DH], F32))
        xn = life.enter_context(nc.sbuf_tensor("xn", [P, NT, D], F32))
        xnT = life.enter_context(nc.sbuf_tensor("xnT", [P, FC, TOK], F32))

        k_parts = dram("k_parts", (3, NH, DH, S), BF16)
        q_parts = dram("q_parts", (3, NH, DH, T), BF16)
        v_heads = dram("v_heads", (B, H, P, NC, VW), F32)
        qk_rot = dram("qk_rot", (2, H, DH, TOK), F32)

        project_queries(nc, a, psum, x_sb, ident, identb, ones_row, neg_half, stats, mv, ve, rstd, xn, xnT, q_parts)
        project_context(nc, a, psum, k_parts, v_heads)
        cross_attention(nc, a, psum, identb, k_parts, q_parts, v_heads, o_all)
        attention_output(nc, "cross", a["xo_w"], a["xo_b"], psum, x_sb, ident, ones_row, o_all, xnT)
        self_attention(nc, a, psum, x_sb, ident, neg_half, stats, mv, ve, rstd, xn, xnT, qk_rot, o_all)
        attention_output(nc, "self", a["so_w"], None, psum, x_sb, ident, ones_row, o_all, xnT)
        experts(nc, a, psum, x_sb, ident, ones_row, neg_half, stats, mv, ve, rstd, xn, xnT, out)


def norm_and_turn(nc, which, psum, x, ident, neg_half, stats, mv, ve, rstd, xn, xnT, ready, done_sem, sem):
    s_stat, s_rstd, s_xn, s_turn = (sem(which + n) for n in ("_stat", "_rstd", "_xn", "_turn"))

    def dve(v):
        ready(v)
        layer_norm_steps(v, nc, s_stat, 0, x, stats, mv, ve)
        v.wait_ge(s_rstd, 1)
        for t in range(NT):
            v.tensor_scalar(xn[:, t, :], x[:, t, :], mv[:, t, 0:1], rstd[:, t:t + 1], ALU.subtract,
                            ALU.mult).then_inc(s_xn, 1)
        for n in range(4):
            v.wait_ge(s_turn, n + 1)
            v.tensor_copy(xnT[:, n // 2, (n % 2) * 512:(n % 2) * 512 + 512], psum[:, n, :]).then_inc(done_sem, 1)

    def pool(g):
        g.wait_ge(s_stat, 3)
        g.tensor_tensor(rstd[:], ve[:], neg_half[:], ALU.pow).then_inc(s_rstd, 1)

    def pe(t_):
        for n in range(4):
            for k in range(4):
                t = 4 * (n % 2) + k
                t_.wait_ge(s_xn, t + 1)
                mm = t_.transpose(psum[:, n, k * P:k * P + P], xn[:, t, (n // 2) * P:(n // 2) * P + P], ident[:])
            mm.then_inc(s_turn, 1)

    return dve, pool, pe


def project_queries(nc, a, psum, x_sb, ident, identb, ones_row, neg_half, stats, mv, ve, rstd, xn, xnT, q_parts):
    with ExitStack() as life:
        def sb(name, shape, dt):
            return life.enter_context(nc.sbuf_tensor(name, shape, dt))

        def sem(name):
            return life.enter_context(nc.semaphore(name))

        wq = sb("wq", [P, FC, D], F32)
        bq = sb("bq", [P, FC], F32)
        q_full = sb("q_full", [P, 4, 512], F32)
        rest = sb("rest", [P, 4, 512], F32)
        parts = sb("parts", [P, 3, 4, 512], BF16)
        s_load, s_const, s_turned, s_q, s_full = (sem(n) for n in ("pq_load", "pq_const", "pq_turned", "pq_q", "pq_full"))
        s_hi, s_rest, s_mid, s_low, s_store = (sem(n) for n in ("pq_hi", "pq_rest", "pq_mid", "pq_low", "pq_store"))
        block = life.enter_context(nc.Block())
        norm_dve, norm_pool, norm_pe = norm_and_turn(
            nc, "ln1", psum, x_sb, ident, neg_half, stats, mv, ve, rstd, xn, xnT,
            lambda v: v.wait_ge(s_load, 16 * 4), s_turned, sem)

        @block.sync
        def _(sp):
            sp.dma_start(x_sb[:], a["x"].rearrange("(t p) d -> p t d", p=P)).then_inc(s_load, 16)
            sp.dma_start(ident[:], a["ident"]).then_inc(s_load, 16)
            sp.dma_start(wq[:], a["xq_w"].rearrange("(c p) n -> p c n", p=P)).then_inc(s_load, 16)
            sp.dma_start(bq[:], a["xq_b"]).then_inc(s_load, 16)
            sp.wait_ge(s_hi, 4)
            sp.wait_ge(s_low, 8)
            for part in range(3):
                for c in range(FC):
                    dst = q_parts[part].rearrange("(b c h) d t -> c (h d) b t", b=B, c=FC)[c]
                    src = parts[:, part, 2 * c:2 * c + 2, :].rearrange("p m (b t) -> p (m b) t", b=2)
                    sp.dma_start(dst, src).then_inc(s_store, 16)
            sp.wait_ge(s_store, 16 * 3 * FC)

        @block.gpsimd
        def _(g):
            g.memset(neg_half[:], -0.5).then_inc(s_const, 1)
            g.memset(ones_row[:], 1.0)
            g.wait_ge(s_const, 1)
            norm_pool(g)

        @block.tensor
        def _(pe):
            norm_pe(pe)
            pe.wait_ge(s_turned, 4)
            for n in range(4):
                for c in range(FC):
                    mm = pe.matmul(psum[:, 4 + n, :], wq[:, c, (n // 2) * P:(n // 2) * P + P],
                                   xnT[:, c, (n % 2) * 512:(n % 2) * 512 + 512], start=(c == 0), stop=(c == FC - 1))
                mm.then_inc(s_q, 1)

        @block.scalar
        def _(act):
            for n in range(4):
                act.wait_ge(s_full, n + 1)
                act.copy(parts[:, 0, n, :], q_full[:, n, :]).then_inc(s_hi, 1)
            for n in range(4):
                act.wait_ge(s_rest, n + 1)
                act.copy(parts[:, 1, n, :], rest[:, n, :]).then_inc(s_mid, 1)

        @block.vector
        def _(v):
            norm_dve(v)
            v.tensor_copy(identb[:], ident[:])
            for n in range(4):
                v.wait_ge(s_q, n + 1)
                v.tensor_scalar(q_full[:, n, :], psum[:, 4 + n, :], bq[:, n // 2:n // 2 + 1], SCALE, ALU.add,
                                ALU.mult).then_inc(s_full, 1)
            for n in range(4):
                v.wait_ge(s_hi, n + 1)
                v.tensor_tensor(rest[:, n, :], q_full[:, n, :], parts[:, 0, n, :], ALU.subtract).then_inc(s_rest, 1)
            for n in range(4):
                v.wait_ge(s_mid, n + 1)
                v.tensor_tensor(parts[:, 2, n, :], rest[:, n, :], parts[:, 1, n, :], ALU.subtract).then_inc(s_low, 2)


def project_context(nc, a, psum, k_parts, v_heads):
    with ExitStack() as life:
        def sb(name, shape, dt):
            return life.enter_context(nc.sbuf_tensor(name, shape, dt))

        def sem(name):
            return life.enter_context(nc.semaphore(name))

        R2 = DC - P
        w_a = sb("w_a", [P, 2, D], F32)
        w_b = sb("w_b", [R2 + 1, 2, D], F32)
        ctx_a = sb("ctx_a", [P, 2, KB], F32)
        ctx_b = sb("ctx_b", [R2 + 1, 2, KB], F32)
        parts = sb("kparts", [P, 2, 3, FC, KB], BF16)
        rest = sb("krest", [P, 2, FC, KB], F32)
        vals = sb("vals", [P, 2, H, 4, VW], F32)
        s_w, s_ones = sem("pc_w"), sem("pc_ones")
        s_ctx = [sem(f"pc_ctx{p}") for p in range(2)]
        s_k, s_v, s_hi, s_rest, s_mid, s_low, s_vals = (
            sem(n) for n in ("pc_k", "pc_v", "pc_hi", "pc_rest", "pc_mid", "pc_low", "pc_vals"))
        s_store = [sem(f"pc_store{p}") for p in range(2)]
        block = life.enter_context(nc.Block())

        def load(sp, n, p):
            sp.dma_start(ctx_a[:, p, :], a["ctxT"][n // 8, 0:P, bass.ds((n % 8) * KB, KB)]).then_inc(s_ctx[p], 16)
            sp.dma_start(ctx_b[0:R2, p, :], a["ctxT"][n // 8, P:DC, bass.ds((n % 8) * KB, KB)]).then_inc(s_ctx[p], 16)

        def store(sp, n, p):
            sp.wait_ge(s_hi, 2 * (n + 1))
            sp.wait_ge(s_mid, 2 * (n + 1))
            sp.wait_ge(s_low, 2 * (n + 1))
            kd = k_parts.rearrange("s (b c h) d t -> b (h d) s c t", b=B, c=FC)
            for c in range(FC):
                sp.dma_start(kd[n // 8, :, :, c, bass.ds((n % 8) * KB, KB)], parts[:, p, :, c, :]).then_inc(s_store[p], 16)
            sp.wait_ge(s_vals, 2 * (n + 1))
            vd = v_heads.rearrange("b h p c w -> b p h (c w)")
            sp.dma_start(vd[n // 8, :, :, bass.ds((n % 8) * 4 * VW, 4 * VW)],
                         vals[:, p].rearrange("p h c w -> p h (c w)")).then_inc(s_store[p], 16)

        @block.sync
        def _(sp):
            sp.dma_start(w_a[:, 0, :], a["xk_w"][0:P]).then_inc(s_w, 16)
            sp.dma_start(w_b[0:R2, 0, :], a["xk_w"][P:DC]).then_inc(s_w, 16)
            sp.dma_start(w_b[R2:R2 + 1, 0, :], a["xk_b"]).then_inc(s_w, 16)
            sp.dma_start(w_a[:, 1, :], a["xv_w"][0:P]).then_inc(s_w, 16)
            sp.dma_start(w_b[0:R2, 1, :], a["xv_w"][P:DC]).then_inc(s_w, 16)
            sp.dma_start(w_b[R2:R2 + 1, 1, :], a["xv_b"]).then_inc(s_w, 16)
            for n in range(2):
                load(sp, n, n)
            with sp.Fori(0, NBLK // 2 - 1) as i:
                for p in range(2):
                    n = 2 * i + p
                    sp.wait_ge(s_v, 2 * (n + 1))
                    load(sp, n + 2, p)
                    store(sp, n, p)
            for n in (NBLK - 2, NBLK - 1):
                store(sp, n, n % 2)
            for p in range(2):
                sp.wait_ge(s_store[p], 48 * (NBLK // 2))

        @block.gpsimd
        def _(g):
            g.memset(ctx_b[R2:R2 + 1, :, :], 1.0).then_inc(s_ones, 1)
            g.wait_ge(s_ones, 1)
            g.memset(vals[:], 1.0).then_inc(s_ones, 1)

        @block.tensor
        def _(pe):
            pe.wait_ge(s_w, 16 * 6)
            pe.wait_ge(s_ones, 2)

            def work(i, p, first):
                n = 2 * i + p
                pe.wait_ge(s_ctx[p], 32 * (i + 1))
                for c in range(FC):
                    if not first:
                        pe.wait_ge(s_rest, 2 * (n - 2) + c + 1)
                    pe.matmul(psum[:, 2 * p + c, :], w_a[:, 0, c * P:c * P + P], ctx_a[:, p, :], start=True, stop=False)
                    pe.matmul(psum[:, 2 * p + c, :], w_b[:, 0, c * P:c * P + P], ctx_b[:, p, :], start=False,
                              stop=True).then_inc(s_k, 1)
                for m in range(2):
                    if not first:
                        pe.wait_ge(s_vals, 2 * (n - 2) + m + 1)
                    for k in range(2):
                        rows = slice((2 * m + k) * P, (2 * m + k) * P + P)
                        bank = psum[:, 4 + 2 * p + m, k * D:k * D + D]
                        pe.matmul(bank, ctx_a[:, p, rows], w_a[:, 1, :], start=True, stop=False)
                        mm = pe.matmul(bank, ctx_b[:, p, rows], w_b[:, 1, :], start=False, stop=True)
                    mm.then_inc(s_v, 1)

            for p in range(2):
                work(0, p, True)
            with pe.Fori(1, NBLK // 2) as i:
                for p in range(2):
                    work(i, p, False)

        @block.scalar
        def _(act):
            act.wait_ge(s_ones, 2)

            def work(i, p, first):
                n = 2 * i + p
                if not first:
                    act.wait_ge(s_store[p], 48 * i)
                for c in range(FC):
                    act.wait_ge(s_k, 2 * n + c + 1)
                    act.copy(parts[:, p, 0, c, :], psum[:, 2 * p + c, :]).then_inc(s_hi, 1)
                for m in range(2):
                    act.wait_ge(s_v, 2 * n + m + 1)
                    act.copy(vals[:, p, :, 2 * m:2 * m + 2, 0:DH],
                             psum[:, 4 + 2 * p + m, :].rearrange("p (c h d) -> p h c d", c=2, h=H)).then_inc(s_vals, 1)
                for c in range(FC):
                    act.wait_ge(s_rest, 2 * n + c + 1)
                    act.copy(parts[:, p, 1, c, :], rest[:, p, c, :]).then_inc(s_mid, 1)

            for p in range(2):
                work(0, p, True)
            with act.Fori(1, NBLK // 2) as i:
                for p in range(2):
                    work(i, p, False)

        @block.vector
        def _(v):
            def work(i, p, first):
                n = 2 * i + p
                for c in range(FC):
                    v.wait_ge(s_hi, 2 * n + c + 1)
                    if not first:
                        v.wait_ge(s_mid, 2 * (n - 2) + c + 1)
                        v.wait_ge(s_low, 2 * (n - 2) + c + 1)
                    v.tensor_tensor(rest[:, p, c, :], psum[:, 2 * p + c, :], parts[:, p, 0, c, :],
                                    ALU.subtract).then_inc(s_rest, 1)
                for c in range(FC):
                    v.wait_ge(s_mid, 2 * n + c + 1)
                    v.tensor_tensor(parts[:, p, 2, c, :], rest[:, p, c, :], parts[:, p, 1, c, :],
                                    ALU.subtract).then_inc(s_low, 1)

            for p in range(2):
                work(0, p, True)
            with v.Fori(1, NBLK // 2) as i:
                for p in range(2):
                    work(i, p, False)


def cross_attention(nc, a, psum, identb, k_parts, q_parts, v_heads, o_all):
    SLOTS = 4
    with ExitStack() as life:
        def sb(name, shape, dt):
            return life.enter_context(nc.sbuf_tensor(name, shape, dt))

        def sem(name):
            return life.enter_context(nc.semaphore(name))

        k_st = [sb(f"k_st{s}", [PARTS + 3, S], BF16) for s in range(SLOTS)]
        q_st = [sb(f"q_st{s}", [PARTS + 3, T], BF16) for s in range(SLOTS)]
        v_st = [sb(f"v_st{s}", [P, NC * VW], F32) for s in range(SLOTS)]
        probs = sb("probs", [P, 2, NC * T], F32)
        mx = sb("mx", [P, 2, 16], F32)
        neg_m = sb("neg_m", [P, 2, 2, 2], F32)
        m_rest = sb("m_rest", [P, 2, 2, 2], F32)
        m_parts = sb("m_parts", [P, 2, 2, 3], BF16)
        pv_sb = sb("pv_sb", [P, T], F32)
        pick = sb("pick", [P, VW], F32)
        recip = sb("recip", [P, 2], F32)
        s_load = [sem(f"xa_load{s}") for s in range(SLOTS)]
        names = ("const", "pick", "m_ready", "m_read", "chain", "parts", "turned", "row", "s_ready", "exp", "clamp",
                 "pv", "pv_read", "o", "o_read", "o_div")
        s = {n: sem("xa_" + n) for n in names}
        NLOAD = 13
        S_BANK, M_BANK, PV_BANK, MISC = 0, 3, 5, 7
        block = life.enter_context(nc.Block())

        def heads(engine, period):
            for r in range(3):
                period(0, r)
            with engine.Fori(0, NH // SLOTS - 1) as i:
                for r in range(3, 3 + SLOTS):
                    period(i, r)
            for r in range(3, 5):
                period(NH // SLOTS - 1, r)

        def flags(i, r):
            h = 4 * i + r
            fixed = isinstance(i, int)
            return h, not fixed or h > 0, not fixed or h < NH, not fixed or h < NH - 1, fixed

        @block.sync
        def _(sp):
            sp.dma_start(pick[:], a["pick"]).then_inc(s["pick"], 16)

            def load(h, slot):
                for g in range(6):
                    rows = slice(g * DH, g * DH + DH)
                    sp.dma_start(k_st[slot][rows, :], k_parts[K_PART[g], h]).then_inc(s_load[slot], 16)
                    sp.dma_start(q_st[slot][rows, :], q_parts[Q_PART[g], h]).then_inc(s_load[slot], 16)
                sp.dma_start(v_st[slot][:], v_heads.rearrange("b h p c w -> (b h) p (c w)")[h]).then_inc(s_load[slot], 16)

            for h in range(SLOTS):
                load(h, h)
            with sp.Fori(1, NH // SLOTS) as i:
                for r in range(SLOTS):
                    h = SLOTS * i + r
                    sp.wait_ge(s["pv"], h - SLOTS + 1)
                    load(h, r)

        @block.gpsimd
        def _(g):
            for k in k_st:
                g.memset(k[PARTS:PARTS + 3, :], 1.0).then_inc(s["const"], 1)

        @block.tensor
        def _(pe):
            def values(h, r, jj):
                par, slot = r % 2, r % SLOTS
                if jj == 0:
                    if not isinstance(h, int) or h >= 2:
                        pe.wait_ge(s["pv_read"], h - 1)
                    else:
                        pe.wait_ge(s["const"], SLOTS + 1)
                pe.wait_ge(s["clamp"], 8 * h + jj + 1)
                for g in range(4):
                    c = 4 * jj + g
                    mm = pe.matmul(psum[32 * g:32 * g + VW, PV_BANK + par, 0:T], v_st[slot][:, c * VW:c * VW + VW],
                                   probs[:, par, c * T:c * T + T], start=(jj == 0), stop=(jj == 7))
                if jj == 7:
                    mm.then_inc(s["pv"], 1)

            def maxima(h, r, i, j):
                slot = r % SLOTS
                if j == 0:
                    pe.wait_ge(s_load[slot], 16 * NLOAD * (i + r // SLOTS + 1))
                if j >= 2 or not isinstance(h, int) or h > 0:
                    pe.wait_ge(s["m_read"], 16 * h + j - 1)
                qc, kb = j // 8, j % 8
                pe.matmul(psum[:, M_BANK + j % 2, :], q_st[slot][0:PARTS, qc * P:qc * P + P],
                          k_st[slot][0:PARTS, kb * 512:kb * 512 + 512], start=True, stop=True).then_inc(s["m_ready"], 1)

            def turn_maxima(h, r):
                pe.wait_ge(s["parts"], h + 1)
                if not isinstance(h, int) or h >= 2:
                    pe.wait_ge(s["o_read"], h - 1)
                for qc in range(2):
                    mm = pe.matmul(psum[96:99, MISC, qc * P:qc * P + P], m_parts[:, r % 2, qc, :], identb[:],
                                   start=True, stop=True)
                mm.then_inc(s["turned"], 1)

            def scores(h, r, j):
                slot = r % SLOTS
                if j == 0:
                    pe.wait_ge(s["row"], h + 1)
                    pe.wait_ge(s["const"], SLOTS)
                if j >= 3:
                    pe.wait_ge(s["exp"], 16 * h + j - 2)
                elif not isinstance(h, int) or h > 0:
                    pe.wait_ge(s["exp"], 16 * h - (0, 2, 1)[j])
                for k in range(2):
                    c = 2 * j + k
                    mm = pe.matmul(psum[:, S_BANK + j % 3, k * T:k * T + T], k_st[slot][:, c * P:c * P + P],
                                   q_st[slot][:, :], start=True, stop=True)
                mm.then_inc(s["s_ready"], 1)

            def output(h):
                pe.wait_ge(s["pv_read"], h + 1)
                if not isinstance(h, int) or h >= 1:
                    pe.wait_ge(s["o_read"], h)
                for qc in range(2):
                    mm = pe.matmul(psum[:, MISC, 256 + qc * VW:256 + qc * VW + VW], pv_sb[:, qc * P:qc * P + P],
                                   pick[:], start=True, stop=True)
                mm.then_inc(s["o"], 1)

            def period(i, r):
                h, before, now, after, fixed = flags(i, r)
                if before:
                    values(h - 1, r - 1, 0)
                    values(h - 1, r - 1, 1)
                if now:
                    turn_maxima(h, r)
                if before:
                    values(h - 1, r - 1, 2)
                    values(h - 1, r - 1, 3)
                for jj in range(8):
                    if now:
                        scores(h, r, 2 * jj)
                        scores(h, r, 2 * jj + 1)
                    if after:
                        maxima(h + 1, r + 1, i, 2 * jj)
                        maxima(h + 1, r + 1, i, 2 * jj + 1)
                    if before and jj < 4:
                        values(h - 1, r - 1, 4 + jj)
                    if before and jj == 6:
                        output(h - 1)

            pe.wait_ge(s["pick"], 16)
            for j in range(16):
                maxima(0, 0, 0, j)
            heads(pe, period)

        @block.scalar
        def _(act):
            def period(i, r):
                h, before, now, after, fixed = flags(i, r)
                if now:
                    act.wait_ge(s["turned"], h + 1)
                    act.copy(q_st[r % SLOTS][96:99, :], psum[96:99, MISC, 0:T]).then_inc(s["row"], 1)
                for j in range(16):
                    if now:
                        act.wait_ge(s["s_ready"], 16 * h + j + 1)
                        if j == 0 and (not fixed or h >= 2):
                            act.wait_ge(s["pv"], h - 1)
                        act.activation(probs[:, r % 2, j * 512:j * 512 + 512], psum[:, S_BANK + j % 3, :],
                                       ACT.Exp).then_inc(s["exp"], 1)
                    if before and j == 10:
                        act.wait_ge(s["pv"], h)
                        if not fixed or h >= 2:
                            act.wait_ge(s["o"], h - 1)
                        act.copy(pv_sb[:], psum[:, PV_BANK + (r - 1) % 2, 0:T]).then_inc(s["pv_read"], 1)

            heads(act, period)

        @block.vector
        def _(v):
            v.memset(psum[:, PV_BANK:PV_BANK + 2, 0:T], 0.0).then_inc(s["const"], 1)

            def row_max(h, r, j):
                v.wait_ge(s["m_ready"], 16 * h + j + 1)
                v.tensor_reduce(mx[:, r % 2, j:j + 1], psum[:, M_BANK + j % 2, :], AX.X, ALU.max).then_inc(s["m_read"], 1)

            def clamp(h, r, jj):
                v.wait_ge(s["exp"], 16 * h + 2 * jj + 2)
                p = probs[:, r % 2, jj * 1024:jj * 1024 + 1024]
                v.tensor_scalar(p, p, 1.0, FLOOR, ALU.min, ALU.max).then_inc(s["clamp"], 1)

            def chain(h, r, step):
                par = r % 2
                if step == 0:
                    v.wait_ge(s["m_read"], 16 * h + 16)
                else:
                    v.wait_ge(s["chain"], 5 * h + step)
                raw, neg, rest = neg_m[:, par, 0], neg_m[:, par, 1], m_rest[:, par, 0]
                hi, mid, low = (m_parts[:, par, :, k] for k in range(3))
                if step == 0:
                    v.tensor_reduce(raw, mx[:, par, :].rearrange("p (q k) -> p q k", q=2), AX.X, ALU.max,
                                    negate=True).then_inc(s["chain"], 1)
                elif step == 1:
                    v.tensor_scalar(neg, raw, CLAMP - LOW, -CLAMP, ALU.min, ALU.max).then_inc(s["chain"], 1)
                elif step == 2:
                    v.tensor_copy(hi, neg).then_inc(s["chain"], 1)
                elif step == 3:
                    v.tensor_tensor(rest, neg, hi, ALU.subtract).then_inc(s["chain"], 1)
                elif step == 4:
                    v.tensor_copy(mid, rest).then_inc(s["chain"], 1)
                else:
                    v.tensor_tensor(low, rest, mid, ALU.subtract).then_inc(s["parts"], 1)

            def finish(h):
                v.wait_ge(s["o"], h + 1)
                o = psum[:, MISC, 256:256 + 2 * VW].rearrange("p (q w) -> p q w", q=2)
                v.reciprocal(recip[:], o[:, :, DH]).then_inc(s["o_div"], 1)
                v.wait_ge(s["o_div"], h + 1)
                v.tensor_tensor(o_all[:, :, bass.ds(h * DH, DH)], o[:, :, 0:DH],
                                recip[:].unsqueeze(2).broadcast_to([P, 2, DH]), ALU.mult).then_inc(s["o_read"], 1)

            def period(i, r):
                h, before, now, after, fixed = flags(i, r)
                for jj in range(8):
                    if after:
                        row_max(h + 1, r + 1, 2 * jj)
                        row_max(h + 1, r + 1, 2 * jj + 1)
                    if after and jj == 7:
                        chain(h + 1, r + 1, 0)
                    if now and jj > 0:
                        clamp(h, r, jj - 1)
                if after:
                    for step in range(1, 6):
                        chain(h + 1, r + 1, step)
                if now:
                    clamp(h, r, 7)
                if before:
                    finish(h - 1)

            for j in range(16):
                row_max(0, 0, j)
            for step in range(6):
                chain(0, 0, step)
            heads(v, period)


def attention_output(nc, which, w_dram, b_dram, psum, x_sb, ident, ones_row, o_all, oT):
    with ExitStack() as life:
        def sb(name, shape, dt):
            return life.enter_context(nc.sbuf_tensor(name, shape, dt))

        def sem(name):
            return life.enter_context(nc.semaphore(name))

        w = sb(which + "_wo", [P, FC, D], F32)
        b = sb(which + "_bo", [1, D], F32)
        s_load, s_turn, s_oT, s_y, s_x = (sem(which + n) for n in ("_load", "_turn", "_oT", "_y", "_x"))
        loads = 1 if b_dram is None else 2
        block = life.enter_context(nc.Block())

        @block.sync
        def _(sp):
            sp.dma_start(w[:], w_dram.rearrange("(c p) n -> p c n", p=P)).then_inc(s_load, 16)
            if b_dram is not None:
                sp.dma_start(b[:], b_dram).then_inc(s_load, 16)

        @block.tensor
        def _(pe):
            pe.wait_ge(s_load, 16 * loads)
            for n in range(4):
                for k in range(4):
                    t = 4 * (n % 2) + k
                    src = o_all[:, t % 2, (t // 2) * D + (n // 2) * P:(t // 2) * D + (n // 2) * P + P]
                    mm = pe.transpose(psum[:, n, k * P:k * P + P], src, ident[:])
                mm.then_inc(s_turn, 1)
            pe.wait_ge(s_oT, 4)
            for t in range(NT):
                bank = psum[:, 4 + t // 2, (t % 2) * D:(t % 2) * D + D]
                for c in range(FC):
                    mm = pe.matmul(bank, oT[:, c, t * P:t * P + P], w[:, c, :], start=(c == 0),
                                   stop=(b_dram is None and c == FC - 1))
                if b_dram is not None:
                    mm = pe.matmul(bank, ones_row[:], b[:], start=False, stop=True)
                if t % 2:
                    mm.then_inc(s_y, 1)

        @block.vector
        def _(v):
            for n in range(4):
                v.wait_ge(s_turn, n + 1)
                v.tensor_copy(oT[:, n // 2, (n % 2) * 512:(n % 2) * 512 + 512], psum[:, n, :]).then_inc(s_oT, 1)
            for m in range(NT // 2):
                v.wait_ge(s_y, m + 1)
                v.tensor_tensor(x_sb[:, 2 * m:2 * m + 2, :], x_sb[:, 2 * m:2 * m + 2, :],
                                psum[:, 4 + m, :].rearrange("p (t d) -> p t d", t=2), ALU.add).then_inc(s_x, 1)


def self_attention(nc, a, psum, x_sb, ident, neg_half, stats, mv, ve, rstd, xn, xnT, qk_rot, o_all):
    with ExitStack() as outer:
        v_all = outer.enter_context(nc.sbuf_tensor("v_all", [P, NT, D], F32))
        with ExitStack() as life:
            def sb(name, shape, dt):
                return life.enter_context(nc.sbuf_tensor(name, shape, dt))

            def sem(name):
                return life.enter_context(nc.semaphore(name))

            w = sb("w_qkv", [P, 5, FC, D], F32)
            cos = sb("cos", [P, 512], F32)
            sin = sb("sin", [P, 512], F32)
            direct = sb("direct", [P, 8, 512], F32)
            swapped = sb("swapped", [P, 8, 512], F32)
            s_load, s_turned, s_mm, s_read, s_add, s_vmm, s_v, s_store = (
                sem(n) for n in ("sp_load", "sp_turned", "sp_mm", "sp_read", "sp_add", "sp_vmm", "sp_v", "sp_store"))
            block = life.enter_context(nc.Block())
            norm_dve, norm_pool, norm_pe = norm_and_turn(
                nc, "ln2", psum, x_sb, ident, neg_half, stats, mv, ve, rstd, xn, xnT, lambda v: None, s_turned, sem)

            @block.sync
            def _(sp):
                for n, name in enumerate(("sq_w", "sk_w", "sq_sw", "sk_sw", "sv_w")):
                    sp.dma_start(w[:, n], a[name].rearrange("(c p) n -> p c n", p=P)).then_inc(s_load, 16)
                sp.dma_start(cos[:], a["cos"]).then_inc(s_load, 16)
                sp.dma_start(sin[:], a["sin"]).then_inc(s_load, 16)
                qk = qk_rot.rearrange("k (c h) d t -> k c (h d) t", c=FC)
                for n in range(8):
                    sp.wait_ge(s_add, n + 1)
                    sp.dma_start(qk[n // 4, (n // 2) % 2, :, (n % 2) * 512:(n % 2) * 512 + 512],
                                 direct[:, n, :]).then_inc(s_store, 16)
                sp.wait_ge(s_store, 16 * 8)

            @block.gpsimd
            def _(g):
                norm_pool(g)

            @block.tensor
            def _(pe):
                norm_pe(pe)
                pe.wait_ge(s_turned, 4)
                pe.wait_ge(s_load, 16 * 7)
                for n in range(8):
                    kind, fo, half = n // 4, (n // 2) % 2, n % 2
                    if n >= 4:
                        pe.wait_ge(s_read, 2 * (n - 4) + 2)
                    for sw in range(2):
                        for c in range(FC):
                            mm = pe.matmul(psum[:, 2 * (n % 4) + sw, :], w[:, 2 * sw + kind, c, fo * P:fo * P + P],
                                           xnT[:, c, half * 512:half * 512 + 512], start=(c == 0), stop=(c == FC - 1))
                    mm.then_inc(s_mm, 1)
                for t in range(NT):
                    if t % 2 == 0:
                        pe.wait_ge(s_read, 2 * (4 + t // 2) + 2)
                    for c in range(FC):
                        mm = pe.matmul(psum[:, t, 0:D], xnT[:, c, t * P:t * P + P], w[:, 4, c, :], start=(c == 0),
                                       stop=(c == FC - 1))
                    mm.then_inc(s_vmm, 1)

            @block.scalar
            def _(act):
                for t in range(NT):
                    act.wait_ge(s_vmm, t + 1)
                    act.copy(v_all[:, t, :], psum[:, t, 0:D]).then_inc(s_v, 1)

            @block.vector
            def _(v):
                norm_dve(v)
                v.wait_ge(s_load, 16 * 7)
                for n in range(8):
                    v.wait_ge(s_mm, n + 1)
                    v.tensor_tensor(direct[:, n, :], psum[:, 2 * (n % 4), :], cos[:], ALU.mult).then_inc(s_read, 1)
                    v.tensor_tensor(swapped[:, n, :], psum[:, 2 * (n % 4) + 1, :], sin[:], ALU.mult).then_inc(s_read, 1)
                    v.wait_ge(s_read, 2 * n + 2)
                    v.tensor_tensor(direct[:, n, :], direct[:, n, :], swapped[:, n, :], ALU.add).then_inc(s_add, 1)

        with ExitStack() as life:
            def sb(name, shape, dt):
                return life.enter_context(nc.sbuf_tensor(name, shape, dt))

            def sem(name):
                return life.enter_context(nc.semaphore(name))

            qk = [sb(f"qk{s}", [DH, 2, T], F32) for s in range(4)]
            vh = [sb(f"vh{s}", [P, 2, DH], F32) for s in range(4)]
            mask = sb("mask", [P, 2 * T], F32)
            masked = sb("masked", [P, 2, 2 * T], F32)
            probs = sb("sprobs", [P, 2, 2, T], F32)
            probsT = sb("probsT", [P, 2, 3, P], F32)
            neg_m = sb("sneg_m", [P, 2, 2], F32)
            total = sb("total", [P, 2, 2], F32)
            recip = sb("srecip", [P, 2], F32)
            total_max = sb("total_max", [P, 2, 2], F32)
            s_raw = sem("sa_raw")
            s_mask = sem("sa_mask")
            s_load = [sem(f"sa_load{s}") for s in range(4)]
            s = {n: sem("sa_" + n) for n in ("s", "masked", "max", "exp", "turn", "pT", "o", "o_div", "o_read")}
            block = life.enter_context(nc.Block())

            @block.sync
            def _(sp):
                sp.dma_start(mask[:], a["mask"]).then_inc(s_mask, 16)

                def load(h, slot):
                    for k in range(2):
                        sp.dma_start(qk[slot][:, k, :], qk_rot[k, h % H, :, bass.ds((h // H) * T, T)]
                                     ).then_inc(s_load[slot], 16)
                    src = v_all[:, bass.ds((h // H) * 2, 2), bass.ds((h % H) * DH, DH)]
                    sp.dma_start(vh[slot][:], src).then_inc(s_load[slot], 16)

                for h in range(4):
                    load(h, h)
                with sp.Fori(1, NH // 4) as i:
                    for r in range(4):
                        sp.wait_ge(s["o"], 4 * i + r - 3)
                        load(4 * i + r, r)

            def periods(engine, step):
                for h in range(4):
                    step(0, h)
                with engine.Fori(1, NH // 4) as i:
                    for r in range(4):
                        step(i, r)
                for r in range(2):
                    step(NH // 4, r)

            def on(i, r, lag):
                h = 4 * i + r - lag
                return h, not isinstance(i, int) or 0 <= h < NH, not isinstance(i, int)

            @block.tensor
            def _(pe):
                def step(i, r):
                    h, live, loop = on(i, r, 0)
                    if live:
                        pe.wait_ge(s_load[r], 48 * (i + 1))
                        if loop or h >= 2:
                            pe.wait_ge(s["masked"], h - 1)
                        for qc in range(2):
                            mm = pe.matmul(psum[:, r % 2, qc * T:qc * T + T], qk[r][:, 0, qc * P:qc * P + P],
                                           qk[r][:, 1, :], start=True, stop=True)
                        mm.then_inc(s["s"], 1)
                    h, live, loop = on(i, r, 1)
                    if live:
                        par = (r - 1) % 2
                        pe.wait_ge(s["exp"], h + 1)
                        if loop or h >= 2:
                            pe.wait_ge(s["pT"], h - 1)
                        for k, (qc, kc) in enumerate(((0, 0), (1, 0), (1, 1))):
                            mm = pe.transpose(psum[:, 2 + par, k * P:k * P + P], probs[:, par, qc, kc * P:kc * P + P],
                                              ident[:])
                        mm.then_inc(s["turn"], 1)
                    h, live, loop = on(i, r, 2)
                    if live:
                        par, slot = r % 2, (r - 2) % 4
                        pe.wait_ge(s["pT"], h + 1)
                        if loop or h >= 2:
                            pe.wait_ge(s["o_read"], h - 1)
                        bank = psum[:, 4 + par, :]
                        pe.matmul(bank[:, 0:DH], probsT[:, par, 0, :], vh[slot][:, 0, :], start=True, stop=True)
                        pe.matmul(bank[:, DH:2 * DH], probsT[:, par, 1, :], vh[slot][:, 0, :], start=True, stop=False)
                        pe.matmul(bank[:, DH:2 * DH], probsT[:, par, 2, :], vh[slot][:, 1, :], start=False,
                                  stop=True).then_inc(s["o"], 1)

                periods(pe, step)

            @block.scalar
            def _(act):
                def step(i, r):
                    h, live, loop = on(i, r, 0)
                    if live:
                        act.wait_ge(s["max"], h + 1)
                        if loop or h >= 2:
                            act.wait_ge(s["turn"], h - 1)
                            act.wait_ge(s["o_div"], h - 1)
                        for qc in range(2):
                            last = act.activation(probs[:, r % 2, qc, :], masked[:, r % 2, qc * T:qc * T + T], ACT.Exp,
                                                  bias=neg_m[:, r % 2, qc:qc + 1], scale=SCALE,
                                                  accum_out=total[:, r % 2, qc:qc + 1])
                        last.then_inc(s["exp"], 1)
                    h, live, loop = on(i, r, 1)
                    if live:
                        par = (r - 1) % 2
                        act.wait_ge(s["turn"], h + 1)
                        if loop or h >= 2:
                            act.wait_ge(s["o"], h - 1)
                        act.copy(probsT[:, par].rearrange("p k q -> p (k q)"), psum[:, 2 + par, 0:3 * P]).then_inc(s["pT"], 1)

                periods(act, step)

            @block.vector
            def _(v):
                v.wait_ge(s_mask, 16)

                def step(i, r):
                    h, live, loop = on(i, r, 0)
                    if live:
                        v.wait_ge(s["s"], h + 1)
                        if loop or h >= 2:
                            v.wait_ge(s["exp"], h - 1)
                        v.tensor_tensor(masked[:, r % 2, :], psum[:, r % 2, :], mask[:], ALU.min).then_inc(s["masked"], 1)
                        v.wait_ge(s["masked"], h + 1)
                        v.tensor_reduce(total_max[:, r % 2, :], masked[:, r % 2, :].rearrange("p (q k) -> p q k", q=2),
                                        AX.X, ALU.max).then_inc(s_raw, 1)
                        v.wait_ge(s_raw, h + 1)
                        v.tensor_scalar(neg_m[:, r % 2, :], total_max[:, r % 2, :], -SCALE, None,
                                        ALU.mult).then_inc(s["max"], 1)
                    h, live, loop = on(i, r, 2)
                    if live:
                        par = r % 2
                        v.wait_ge(s["o"], h + 1)
                        if loop or h >= 1:
                            v.wait_ge(s["o_read"], h)
                        v.reciprocal(recip[:], total[:, par, :]).then_inc(s["o_div"], 1)
                        v.wait_ge(s["o_div"], h + 1)
                        o = psum[:, 4 + par, 0:2 * DH].rearrange("p (q d) -> p q d", q=2)
                        v.tensor_tensor(o_all[:, :, bass.ds(h * DH, DH)], o,
                                        recip[:].unsqueeze(2).broadcast_to([P, 2, DH]), ALU.mult).then_inc(s["o_read"], 1)

                periods(v, step)


def experts(nc, a, psum, x_sb, ident, ones_row, neg_half, stats, mv, ve, rstd, xn, xnT, out):
    with ExitStack() as life:
        def sb(name, shape, dt):
            return life.enter_context(nc.sbuf_tensor(name, shape, dt))

        def sem(name):
            return life.enter_context(nc.semaphore(name))

        wr = sb("wr", [P, FC, E], F32)
        br = sb("br", [1, E], F32)
        b1 = sb("b1", [P, E, HC], F32)
        b2 = sb("b2", [E, D], F32)
        w1 = [sb(f"w1_{p}", [P, FC, HID], F32) for p in range(2)]
        w2 = [sb(f"w2_{p}", [P, HC, D], F32) for p in range(2)]
        hid = sb("hid", [P, HC, TOK], F32)
        logits = sb("logits", [P, NT, E], F32)
        top = sb("top", [P, NT, 8], F32)
        shifted = sb("shifted", [P, NT, E], F32)
        gate = sb("gate", [P, NT, E], F32)
        gates = sb("gates", [P, NT, E], F32)
        gsum = sb("gsum", [P, NT], F32)
        grec = sb("grec", [P, NT], F32)
        gatesT = sb("gatesT", [E, TOK], F32)
        acc = sb("acc", [P, NT, D], F32)
        b1_cur = sb("b1_cur", [P, 2, HC], F32)
        gate_cur = sb("gate_cur", [P, 2, NT], F32)
        s_b1, s_acc0b, s_gc = sem("ex_b1"), sem("ex_rec"), sem("ex_gate")
        s_load, s_turned, s_log, s_g, s_gexp, s_gT, s_gTc, s_b2, s_acc0 = (
            sem(n) for n in ("ex_load", "ex_turned", "ex_log", "ex_g", "ex_gexp", "ex_gT", "ex_gTc", "ex_b2", "ex_acc0"))
        s_w = [sem(f"ex_w{p}") for p in range(2)]
        s_up, s_gelu, s_down, s_acc, s_out = (sem(n) for n in ("ex_up", "ex_gelu", "ex_down", "ex_acc", "ex_out"))
        block = life.enter_context(nc.Block())
        norm_dve, norm_pool, norm_pe = norm_and_turn(
            nc, "ln3", psum, x_sb, ident, neg_half, stats, mv, ve, rstd, xn, xnT, lambda v: None, s_turned, sem)

        def load(sp, e, p):
            sp.dma_start(w1[p][:], a["e1_w"][e].rearrange("(c p) n -> p c n", p=P)).then_inc(s_w[p], 16)
            sp.dma_start(w2[p][:], a["e2_w"][e].rearrange("(c p) n -> p c n", p=P)).then_inc(s_w[p], 16)

        @block.sync
        def _(sp):
            sp.dma_start(wr[:], a["r_w"].rearrange("(c p) n -> p c n", p=P)).then_inc(s_load, 16)
            sp.dma_start(br[:], a["r_b"]).then_inc(s_load, 16)
            sp.dma_start(b1[:], a["e1_b"]).then_inc(s_load, 16)
            sp.dma_start(b2[:], a["e2_b"]).then_inc(s_load, 16)
            load(sp, 0, 0)
            load(sp, 1, 1)
            with sp.Fori(1, E // 2) as i:
                for p in range(2):
                    sp.wait_ge(s_down, NT * (2 * i + p - 1))
                    load(sp, 2 * i + p, p)
            sp.wait_ge(s_acc, NT * E)
            sp.dma_start(out.rearrange("(t p) d -> p t d", p=P), acc[:]).then_inc(s_out, 16)
            sp.wait_ge(s_out, 16)

        @block.gpsimd
        def _(g):
            norm_pool(g)

        @block.tensor
        def _(pe):
            norm_pe(pe)
            pe.wait_ge(s_turned, 4)
            pe.wait_ge(s_load, 64)
            for t in range(NT):
                bank = psum[:, 4, t * E:t * E + E]
                for c in range(FC):
                    pe.matmul(bank, xnT[:, c, t * P:t * P + P], wr[:, c, :], start=(c == 0), stop=False)
                mm = pe.matmul(bank, ones_row[:], br[:], start=False, stop=True)
            mm.then_inc(s_log, 1)
            pe.wait_ge(s_g, 7)
            for t in range(NT):
                mm = pe.transpose(psum[0:E, 5 + t // 4, (t % 4) * P:(t % 4) * P + P], gates[:, t, :], ident[:])
            mm.then_inc(s_gT, 1)
            pe.wait_ge(s_gTc, 1)
            for t in range(NT):
                mm = pe.matmul(psum[:, t // 2, (t % 2) * D:(t % 2) * D + D], gatesT[:, t * P:t * P + P], b2[:],
                               start=True, stop=True)
            mm.then_inc(s_b2, 1)
            pe.wait_ge(s_acc0, 1)

            def expert(i, p, first):
                e = 2 * i + p
                pe.wait_ge(s_w[p], 32 * (i + 1))
                for n in range(2 * HC):
                    if n >= 4:
                        pe.wait_ge(s_gelu, 2 * HC * e + n - 3)
                    elif not first:
                        pe.wait_ge(s_gelu, 2 * HC * e + n - 3)
                    for c in range(FC):
                        mm = pe.matmul(psum[:, n % 4, :], w1[p][:, c, (n // 2) * P:(n // 2) * P + P],
                                       xnT[:, c, (n % 2) * 512:(n % 2) * 512 + 512], start=(c == 0), stop=(c == FC - 1))
                    mm.then_inc(s_up, 1)
                pe.wait_ge(s_gelu, 2 * HC * (e + 1))
                for t in range(NT):
                    if t >= 4 or not first:
                        pe.wait_ge(s_acc, NT * e + t - 3)
                    for c in range(HC):
                        mm = pe.matmul(psum[:, 4 + t % 4, 0:D], hid[:, c, t * P:t * P + P], w2[p][:, c, :],
                                       start=(c == 0), stop=(c == HC - 1))
                    mm.then_inc(s_down, 1)

            expert(0, 0, True)
            expert(0, 1, False)
            with pe.Fori(1, E // 2) as i:
                for p in range(2):
                    expert(i, p, False)

        @block.scalar
        def _(act):
            act.wait_ge(s_g, 4)
            act.activation(gate[:], shifted[:], ACT.Exp).then_inc(s_gexp, 1)

            def expert(i, p, first):
                e = 2 * i + p
                for n in range(2 * HC):
                    act.wait_ge(s_up, 2 * HC * e + n + 1)
                    if n == 0 and not first:
                        act.wait_ge(s_down, NT * e)
                    act.activation(hid[:, n // 2, (n % 2) * 512:(n % 2) * 512 + 512], psum[:, n % 4, :], ACT.Gelu,
                                   bias=b1_cur[:, p, n // 2:n // 2 + 1]).then_inc(s_gelu, 1)

            def bias(i, p, first):
                if not first:
                    act.wait_ge(s_gelu, 2 * HC * (2 * i + p))
                act.copy(b1_cur[:, p, :], b1[:, 2 * i + p, :]).then_inc(s_b1, 1)
                act.wait_ge(s_b1, 2 * i + p + 1)

            act.wait_ge(s_load, 64)
            for p in range(2):
                bias(0, p, p == 0)
                expert(0, p, p == 0)
            with act.Fori(1, E // 2) as i:
                for p in range(2):
                    bias(i, p, False)
                    expert(i, p, False)

        @block.vector
        def _(v):
            norm_dve(v)
            v.wait_ge(s_log, 1)
            v.tensor_copy(logits[:], psum[:, 4, 0:NT * E].rearrange("p (t e) -> p t e", t=NT)).then_inc(s_g, 1)
            v.wait_ge(s_g, 1)
            for t in range(NT):
                last = v.max(top[:, t, :], logits[:, t, :])
            last.then_inc(s_g, 1)
            v.wait_ge(s_g, 2)
            v.tensor_tensor(gates[:], logits[:], top[:, :, 1:2].broadcast_to([P, NT, E]), ALU.is_ge).then_inc(s_g, 1)
            v.tensor_tensor(shifted[:], logits[:], top[:, :, 0:1].broadcast_to([P, NT, E]),
                            ALU.subtract).then_inc(s_g, 1)
            v.wait_ge(s_gexp, 1)
            v.wait_ge(s_g, 4)
            v.tensor_tensor(gate[:], gate[:], gates[:], ALU.mult).then_inc(s_g, 1)
            v.wait_ge(s_g, 5)
            v.tensor_reduce(gsum[:], gate[:], AX.X, ALU.add).then_inc(s_g, 1)
            v.wait_ge(s_g, 6)
            v.reciprocal(grec[:], gsum[:]).then_inc(s_acc0b, 1)
            v.wait_ge(s_acc0b, 1)
            v.tensor_tensor(gates[:], gate[:], grec[:].unsqueeze(2).broadcast_to([P, NT, E]), ALU.mult).then_inc(s_g, 1)
            v.wait_ge(s_gT, 1)
            v.tensor_copy(gatesT[:].rearrange("e (a t) -> e a t", a=2), psum[0:E, 5:7, :]).then_inc(s_gTc, 1)
            v.wait_ge(s_b2, 1)
            v.wait_ge(s_g, 7)
            v.tensor_tensor(acc[:], x_sb[:], psum[:, 0:4, :].rearrange("p a (t d) -> p (a t) d", t=2),
                            ALU.add).then_inc(s_acc0, 1)
            v.wait_ge(s_acc0, 1)

            def expert(i, p):
                e = 2 * i + p
                v.tensor_copy(gate_cur[:, p, :], gates[:, :, bass.ds(e, 1)].rearrange("p t o -> p (t o)")).then_inc(s_gc, 1)
                v.wait_ge(s_gc, e + 1)
                for t in range(NT):
                    v.wait_ge(s_down, NT * e + t + 1)
                    v.scalar_tensor_tensor(out=acc[:, t, :], in0=psum[:, 4 + t % 4, 0:D], scalar=gate_cur[:, p, t:t + 1],
                                           in1=acc[:, t, :], op0=ALU.mult, op1=ALU.add).then_inc(s_acc, 1)

            expert(0, 0)
            expert(0, 1)
            with v.Fori(1, E // 2) as i:
                for p in range(2):
                    expert(i, p)


def constants():
    inv = 1.0 / np.float32(10000.0) ** (np.arange(0, DH, 2, dtype=np.float32) / DH)
    ang = np.arange(T, dtype=np.float32)[:, None] * inv[None, :].astype(np.float32)
    cos = np.concatenate([np.cos(ang), np.cos(ang)], -1).T
    sin = np.concatenate([-np.sin(ang), np.sin(ang)], -1).T
    big = np.float32(3e38)
    mask = np.full((P, 2, T), big, np.float32)
    for qc in range(2):
        mask[:, qc][np.arange(T)[None, :] > (qc * P + np.arange(P))[:, None]] = -big
    pick = np.zeros((P, VW), np.float32)
    for g in range(4):
        pick[32 * g + np.arange(VW), np.arange(VW)] = 1.0
    return {
        "ident": np.eye(P, dtype=np.float32), "pick": pick, "mask": mask.reshape(P, 2 * T),
        "cos": np.tile(cos, (P // DH, 2)).astype(np.float32), "sin": np.tile(sin, (P // DH, 2)).astype(np.float32),
    }


def kernel(x, ctx_768, L0_xattn_Wq, L0_xattn_bq, L0_xattn_Wk, L0_xattn_bk, L0_xattn_Wv, L0_xattn_bv, L0_xattn_Wo,
           L0_xattn_bo, L0_attn_Wq, L0_attn_Wk, L0_attn_Wv, L0_attn_Wo, L0_ffn_W1, L0_ffn_b1, L0_ffn_W2, L0_ffn_b2,
           L0_ffn_Wr, L0_ffn_br):
    import concourse.bacc as _bacc
    from concourse.bass_utils import run_bass_kernel_spmd as _run

    def swap(w):
        return np.asarray(w).reshape(H, 2, DH // 2, D)[:, ::-1].reshape(D, D)

    arrays = {
        "x": np.asarray(x).reshape(TOK, D), "ctxT": np.asarray(ctx_768).transpose(0, 2, 1),
        "xq_w": L0_xattn_Wq, "xq_b": np.asarray(L0_xattn_bq).reshape(FC, P).T, "xk_w": L0_xattn_Wk,
        "xk_b": np.asarray(L0_xattn_bk).reshape(1, D), "xv_w": L0_xattn_Wv, "xv_b": np.asarray(L0_xattn_bv).reshape(1, D),
        "xo_w": L0_xattn_Wo, "xo_b": np.asarray(L0_xattn_bo).reshape(1, D),
        "sq_w": np.asarray(L0_attn_Wq).T, "sk_w": np.asarray(L0_attn_Wk).T, "sq_sw": swap(L0_attn_Wq).T,
        "sk_sw": swap(L0_attn_Wk).T, "sv_w": np.asarray(L0_attn_Wv).T, "so_w": np.asarray(L0_attn_Wo).T,
        "r_w": L0_ffn_Wr, "r_b": np.asarray(L0_ffn_br).reshape(1, E), "e1_w": L0_ffn_W1,
        "e1_b": np.asarray(L0_ffn_b1).reshape(E, HC, P).transpose(2, 0, 1), "e2_w": L0_ffn_W2, "e2_b": L0_ffn_b2,
        **constants(),
    }
    arrays = {name: np.ascontiguousarray(v) for name, v in arrays.items()}
    nc = _bacc.Bacc("TRN2", target_bir_lowering=False, num_devices=1)
    args = {name: nc.dram_tensor("in_" + name, v.shape, mybir.dt.from_np(v.dtype), kind="ExternalInput").ap()
            for name, v in arrays.items()}
    out = nc.dram_tensor("out", (TOK, D), F32, kind="ExternalOutput").ap()
    build_program(nc, args, out)
    r = _run(nc, [{"in_" + name: v for name, v in arrays.items()}], core_ids=[0])
    return r.results[0]["out"].reshape(B, T, D)
```

```python
from contextlib import ExitStack

import numpy as np

import concourse.bass as bass
from concourse import mybir

F32 = mybir.dt.float32
BF16 = mybir.dt.bfloat16
ALU = mybir.AluOpType
ACT = mybir.ActivationFunctionType
AX = mybir.AxisListType

P = 128
B, T, D = 4, 256, 256
S, DC = 4096, 192
H = 16
DH = D // H
NH = B * H
TOK = B * T
NT = TOK // P
FC = D // P
E, HID = 8, 1024
HC = HID // P
KB = 512
NBLK = B * S // KB
NC = S // P
VW = DH + 1
PARTS = 6 * DH
K_PART = (0, 0, 0, 1, 1, 2)
Q_PART = (0, 1, 2, 0, 1, 0)
SCALE = DH ** -0.5
CLAMP = 10000.0
EPS = 1e-5
LOW = 64.0
FLOOR = float(np.exp(-LOW))


def layer_norm_steps(dve, nc, sem, base, x, stats, mv, ve, first=None):
    for t in range(NT):
        last = dve.bn_stats(stats[:, t, :], x[:, t, :])
    last.then_inc(sem, 1)
    dve.wait_ge(sem, base + 1)
    for t in range(NT):
        last = dve.bn_aggr(mv[:, t, :], stats[:, t, :])
    last.then_inc(sem, 1)
    dve.wait_ge(sem, base + 2)
    dve.tensor_scalar(ve[:], mv[:, :, 1], EPS, None, ALU.add).then_inc(sem, 1)


def build_program(nc, a, out):
    with ExitStack() as life:
        def dram(name, shape, dt):
            return nc.dram_tensor(name, shape, dt).ap()

        def sem(name):
            return life.enter_context(nc.semaphore(name))

        psum = life.enter_context(nc.psum_tensor("psum", [P, 8, 512], F32))
        x_sb = life.enter_context(nc.sbuf_tensor("x_sb", [P, NT, D], F32))
        ident = life.enter_context(nc.sbuf_tensor("ident", [P, P], F32))
        identb = life.enter_context(nc.sbuf_tensor("identb", [P, P], BF16))
        ones_row = life.enter_context(nc.sbuf_tensor("ones_row", [1, P], F32))
        neg_half = life.enter_context(nc.sbuf_tensor("neg_half", [P, NT], F32))
        stats = life.enter_context(nc.sbuf_tensor("stats", [P, NT, 6], F32))
        mv = life.enter_context(nc.sbuf_tensor("mv", [P, NT, 2], F32))
        ve = life.enter_context(nc.sbuf_tensor("ve", [P, NT], F32))
        rstd = life.enter_context(nc.sbuf_tensor("rstd", [P, NT], F32))
        o_all = life.enter_context(nc.sbuf_tensor("o_all", [P, FC, NH * DH], F32))
        xn = life.enter_context(nc.sbuf_tensor("xn", [P, NT, D], F32))
        xnT = life.enter_context(nc.sbuf_tensor("xnT", [P, FC, TOK], F32))

        k_parts = dram("k_parts", (3, NH, DH, S), BF16)
        q_parts = dram("q_parts", (3, NH, DH, T), BF16)
        v_heads = dram("v_heads", (B, H, P, NC, VW), F32)
        qk_rot = dram("qk_rot", (2, H, DH, TOK), F32)

        project_queries(nc, a, psum, x_sb, ident, identb, ones_row, neg_half, stats, mv, ve, rstd, xn, xnT, q_parts)
        project_context(nc, a, psum, k_parts, v_heads)
        cross_attention(nc, a, psum, identb, k_parts, q_parts, v_heads, o_all)
        attention_output(nc, "cross", a["xo_w"], a["xo_b"], psum, x_sb, ident, ones_row, o_all, xnT)
        self_attention(nc, a, psum, x_sb, ident, neg_half, stats, mv, ve, rstd, xn, xnT, qk_rot, o_all)
        attention_output(nc, "self", a["so_w"], None, psum, x_sb, ident, ones_row, o_all, xnT)
        experts(nc, a, psum, x_sb, ident, ones_row, neg_half, stats, mv, ve, rstd, xn, xnT, out)


def norm_and_turn(nc, which, psum, x, ident, neg_half, stats, mv, ve, rstd, xn, xnT, ready, done_sem, sem):
    s_stat, s_rstd, s_xn, s_turn = (sem(which + n) for n in ("_stat", "_rstd", "_xn", "_turn"))

    def dve(v):
        ready(v)
        layer_norm_steps(v, nc, s_stat, 0, x, stats, mv, ve)
        v.wait_ge(s_rstd, 1)
        for t in range(NT):
            v.tensor_scalar(xn[:, t, :], x[:, t, :], mv[:, t, 0:1], rstd[:, t:t + 1], ALU.subtract,
                            ALU.mult).then_inc(s_xn, 1)
        for n in range(4):
            v.wait_ge(s_turn, n + 1)
            v.tensor_copy(xnT[:, n // 2, (n % 2) * 512:(n % 2) * 512 + 512], psum[:, n, :]).then_inc(done_sem, 1)

    def pool(g):
        g.wait_ge(s_stat, 3)
        g.tensor_tensor(rstd[:], ve[:], neg_half[:], ALU.pow).then_inc(s_rstd, 1)

    def pe(t_):
        for n in range(4):
            for k in range(4):
                t = 4 * (n % 2) + k
                t_.wait_ge(s_xn, t + 1)
                mm = t_.transpose(psum[:, n, k * P:k * P + P], xn[:, t, (n // 2) * P:(n // 2) * P + P], ident[:])
            mm.then_inc(s_turn, 1)

    return dve, pool, pe


def project_queries(nc, a, psum, x_sb, ident, identb, ones_row, neg_half, stats, mv, ve, rstd, xn, xnT, q_parts):
    with ExitStack() as life:
        def sb(name, shape, dt):
            return life.enter_context(nc.sbuf_tensor(name, shape, dt))

        def sem(name):
            return life.enter_context(nc.semaphore(name))

        wq = sb("wq", [P, FC, D], F32)
        bq = sb("bq", [P, FC], F32)
        q_full = sb("q_full", [P, 4, 512], F32)
        rest = sb("rest", [P, 4, 512], F32)
        parts = sb("parts", [P, 3, 4, 512], BF16)
        s_load, s_const, s_turned, s_q, s_full = (sem(n) for n in ("pq_load", "pq_const", "pq_turned", "pq_q", "pq_full"))
        s_hi, s_rest, s_mid, s_low, s_store = (sem(n) for n in ("pq_hi", "pq_rest", "pq_mid", "pq_low", "pq_store"))
        block = life.enter_context(nc.Block())
        norm_dve, norm_pool, norm_pe = norm_and_turn(
            nc, "ln1", psum, x_sb, ident, neg_half, stats, mv, ve, rstd, xn, xnT,
            lambda v: v.wait_ge(s_load, 16 * 4), s_turned, sem)

        @block.sync
        def _(sp):
            sp.dma_start(x_sb[:], a["x"].rearrange("(t p) d -> p t d", p=P)).then_inc(s_load, 16)
            sp.dma_start(ident[:], a["ident"]).then_inc(s_load, 16)
            sp.dma_start(wq[:], a["xq_w"].rearrange("(c p) n -> p c n", p=P)).then_inc(s_load, 16)
            sp.dma_start(bq[:], a["xq_b"]).then_inc(s_load, 16)
            sp.wait_ge(s_hi, 4)
            sp.wait_ge(s_low, 8)
            for part in range(3):
                for c in range(FC):
                    dst = q_parts[part].rearrange("(b c h) d t -> c (h d) b t", b=B, c=FC)[c]
                    src = parts[:, part, 2 * c:2 * c + 2, :].rearrange("p m (b t) -> p (m b) t", b=2)
                    sp.dma_start(dst, src).then_inc(s_store, 16)
            sp.wait_ge(s_store, 16 * 3 * FC)

        @block.gpsimd
        def _(g):
            g.memset(neg_half[:], -0.5).then_inc(s_const, 1)
            g.memset(ones_row[:], 1.0)
            g.wait_ge(s_const, 1)
            norm_pool(g)

        @block.tensor
        def _(pe):
            norm_pe(pe)
            pe.wait_ge(s_turned, 4)
            for n in range(4):
                for c in range(FC):
                    mm = pe.matmul(psum[:, 4 + n, :], wq[:, c, (n // 2) * P:(n // 2) * P + P],
                                   xnT[:, c, (n % 2) * 512:(n % 2) * 512 + 512], start=(c == 0), stop=(c == FC - 1))
                mm.then_inc(s_q, 1)

        @block.scalar
        def _(act):
            for n in range(4):
                act.wait_ge(s_full, n + 1)
                act.copy(parts[:, 0, n, :], q_full[:, n, :]).then_inc(s_hi, 1)
            for n in range(4):
                act.wait_ge(s_rest, n + 1)
                act.copy(parts[:, 1, n, :], rest[:, n, :]).then_inc(s_mid, 1)

        @block.vector
        def _(v):
            norm_dve(v)
            v.tensor_copy(identb[:], ident[:])
            for n in range(4):
                v.wait_ge(s_q, n + 1)
                v.tensor_scalar(q_full[:, n, :], psum[:, 4 + n, :], bq[:, n // 2:n // 2 + 1], SCALE, ALU.add,
                                ALU.mult).then_inc(s_full, 1)
            for n in range(4):
                v.wait_ge(s_hi, n + 1)
                v.tensor_tensor(rest[:, n, :], q_full[:, n, :], parts[:, 0, n, :], ALU.subtract).then_inc(s_rest, 1)
            for n in range(4):
                v.wait_ge(s_mid, n + 1)
                v.tensor_tensor(parts[:, 2, n, :], rest[:, n, :], parts[:, 1, n, :], ALU.subtract).then_inc(s_low, 2)


def project_context(nc, a, psum, k_parts, v_heads):
    with ExitStack() as life:
        def sb(name, shape, dt):
            return life.enter_context(nc.sbuf_tensor(name, shape, dt))

        def sem(name):
            return life.enter_context(nc.semaphore(name))

        R2 = DC - P
        w_a = sb("w_a", [P, 2, D], F32)
        w_b = sb("w_b", [R2 + 1, 2, D], F32)
        ctx_a = sb("ctx_a", [P, 2, KB], F32)
        ctx_b = sb("ctx_b", [R2 + 1, 2, KB], F32)
        parts = sb("kparts", [P, 2, 3, FC, KB], BF16)
        rest = sb("krest", [P, 2, FC, KB], F32)
        vals = sb("vals", [P, 2, H, 4, VW], F32)
        s_w, s_ones = sem("pc_w"), sem("pc_ones")
        s_ctx = [sem(f"pc_ctx{p}") for p in range(2)]
        s_k, s_v, s_hi, s_rest, s_mid, s_low, s_vals = (
            sem(n) for n in ("pc_k", "pc_v", "pc_hi", "pc_rest", "pc_mid", "pc_low", "pc_vals"))
        s_store = [sem(f"pc_store{p}") for p in range(2)]
        block = life.enter_context(nc.Block())

        def load(sp, n, p):
            sp.dma_start(ctx_a[:, p, :], a["ctxT"][n // 8, 0:P, bass.ds((n % 8) * KB, KB)]).then_inc(s_ctx[p], 16)
            sp.dma_start(ctx_b[0:R2, p, :], a["ctxT"][n // 8, P:DC, bass.ds((n % 8) * KB, KB)]).then_inc(s_ctx[p], 16)

        def store(sp, n, p):
            sp.wait_ge(s_hi, 2 * (n + 1))
            sp.wait_ge(s_mid, 2 * (n + 1))
            sp.wait_ge(s_low, 2 * (n + 1))
            kd = k_parts.rearrange("s (b c h) d t -> b (h d) s c t", b=B, c=FC)
            for c in range(FC):
                sp.dma_start(kd[n // 8, :, :, c, bass.ds((n % 8) * KB, KB)], parts[:, p, :, c, :]).then_inc(s_store[p], 16)
            sp.wait_ge(s_vals, 2 * (n + 1))
            vd = v_heads.rearrange("b h p c w -> b p h (c w)")
            sp.dma_start(vd[n // 8, :, :, bass.ds((n % 8) * 4 * VW, 4 * VW)],
                         vals[:, p].rearrange("p h c w -> p h (c w)")).then_inc(s_store[p], 16)

        @block.sync
        def _(sp):
            sp.dma_start(w_a[:, 0, :], a["xk_w"][0:P]).then_inc(s_w, 16)
            sp.dma_start(w_b[0:R2, 0, :], a["xk_w"][P:DC]).then_inc(s_w, 16)
            sp.dma_start(w_b[R2:R2 + 1, 0, :], a["xk_b"]).then_inc(s_w, 16)
            sp.dma_start(w_a[:, 1, :], a["xv_w"][0:P]).then_inc(s_w, 16)
            sp.dma_start(w_b[0:R2, 1, :], a["xv_w"][P:DC]).then_inc(s_w, 16)
            sp.dma_start(w_b[R2:R2 + 1, 1, :], a["xv_b"]).then_inc(s_w, 16)
            for n in range(2):
                load(sp, n, n)
            with sp.Fori(0, NBLK // 2 - 1) as i:
                for p in range(2):
                    n = 2 * i + p
                    sp.wait_ge(s_v, 2 * (n + 1))
                    load(sp, n + 2, p)
                    store(sp, n, p)
            for n in (NBLK - 2, NBLK - 1):
                store(sp, n, n % 2)
            for p in range(2):
                sp.wait_ge(s_store[p], 48 * (NBLK // 2))

        @block.gpsimd
        def _(g):
            g.memset(ctx_b[R2:R2 + 1, :, :], 1.0).then_inc(s_ones, 1)
            g.wait_ge(s_ones, 1)
            g.memset(vals[:], 1.0).then_inc(s_ones, 1)

        @block.tensor
        def _(pe):
            pe.wait_ge(s_w, 16 * 6)
            pe.wait_ge(s_ones, 2)

            def work(i, p, first):
                n = 2 * i + p
                pe.wait_ge(s_ctx[p], 32 * (i + 1))
                for c in range(FC):
                    if not first:
                        pe.wait_ge(s_rest, 2 * (n - 2) + c + 1)
                    pe.matmul(psum[:, 2 * p + c, :], w_a[:, 0, c * P:c * P + P], ctx_a[:, p, :], start=True, stop=False)
                    pe.matmul(psum[:, 2 * p + c, :], w_b[:, 0, c * P:c * P + P], ctx_b[:, p, :], start=False,
                              stop=True).then_inc(s_k, 1)
                for m in range(2):
                    if not first:
                        pe.wait_ge(s_vals, 2 * (n - 2) + m + 1)
                    for k in range(2):
                        rows = slice((2 * m + k) * P, (2 * m + k) * P + P)
                        bank = psum[:, 4 + 2 * p + m, k * D:k * D + D]
                        pe.matmul(bank, ctx_a[:, p, rows], w_a[:, 1, :], start=True, stop=False)
                        mm = pe.matmul(bank, ctx_b[:, p, rows], w_b[:, 1, :], start=False, stop=True)
                    mm.then_inc(s_v, 1)

            for p in range(2):
                work(0, p, True)
            with pe.Fori(1, NBLK // 2) as i:
                for p in range(2):
                    work(i, p, False)

        @block.scalar
        def _(act):
            act.wait_ge(s_ones, 2)

            def work(i, p, first):
                n = 2 * i + p
                if not first:
                    act.wait_ge(s_store[p], 48 * i)
                for c in range(FC):
                    act.wait_ge(s_k, 2 * n + c + 1)
                    act.copy(parts[:, p, 0, c, :], psum[:, 2 * p + c, :]).then_inc(s_hi, 1)
                for m in range(2):
                    act.wait_ge(s_v, 2 * n + m + 1)
                    act.copy(vals[:, p, :, 2 * m:2 * m + 2, 0:DH],
                             psum[:, 4 + 2 * p + m, :].rearrange("p (c h d) -> p h c d", c=2, h=H)).then_inc(s_vals, 1)
                for c in range(FC):
                    act.wait_ge(s_rest, 2 * n + c + 1)
                    act.copy(parts[:, p, 1, c, :], rest[:, p, c, :]).then_inc(s_mid, 1)

            for p in range(2):
                work(0, p, True)
            with act.Fori(1, NBLK // 2) as i:
                for p in range(2):
                    work(i, p, False)

        @block.vector
        def _(v):
            def work(i, p, first):
                n = 2 * i + p
                for c in range(FC):
                    v.wait_ge(s_hi, 2 * n + c + 1)
                    if not first:
                        v.wait_ge(s_mid, 2 * (n - 2) + c + 1)
                        v.wait_ge(s_low, 2 * (n - 2) + c + 1)
                    v.tensor_tensor(rest[:, p, c, :], psum[:, 2 * p + c, :], parts[:, p, 0, c, :],
                                    ALU.subtract).then_inc(s_rest, 1)
                for c in range(FC):
                    v.wait_ge(s_mid, 2 * n + c + 1)
                    v.tensor_tensor(parts[:, p, 2, c, :], rest[:, p, c, :], parts[:, p, 1, c, :],
                                    ALU.subtract).then_inc(s_low, 1)

            for p in range(2):
                work(0, p, True)
            with v.Fori(1, NBLK // 2) as i:
                for p in range(2):
                    work(i, p, False)


def cross_attention(nc, a, psum, identb, k_parts, q_parts, v_heads, o_all):
    BUFS = 4
    with ExitStack() as life:
        def sb(name, shape, dt):
            return life.enter_context(nc.sbuf_tensor(name, shape, dt))

        def sem(name):
            return life.enter_context(nc.semaphore(name))

        ROWS = PARTS + 4
        k_st = [sb(f"k_st{n}", [ROWS, S], BF16) for n in range(BUFS)]
        q_st = [sb(f"q_st{n}", [ROWS, T], BF16) for n in range(BUFS)]
        v_st = [sb(f"v_st{n}", [P, NC * VW], F32) for n in range(BUFS)]
        probs = sb("probs", [P, 2, NC * T], F32)
        mx = sb("mx", [P, 2, 8], F32)
        raw_m = sb("raw_m", [P, 2], F32)
        neg_m = sb("neg_m", [P, 2], F32)
        m_rest = sb("m_rest", [P, 2], F32)
        m_parts = sb("m_parts", [P, 2, 4], BF16)
        flag = sb("flag", [P, 2], mybir.dt.int32)
        pv_sb = sb("pv_sb", [P, T], F32)
        pick = sb("pick", [P, VW], F32)
        recip = sb("recip", [P, 2], F32)
        spare = sb("spare", [1, 4], F32)
        s_kq = [sem(f"xa_kq{n}") for n in range(BUFS)]
        s_vl = [sem(f"xa_vl{n}") for n in range(BUFS)]
        names = ("const", "pick", "m_ready", "m_read", "raw", "neg", "high", "rest", "mid", "parts", "turned", "row",
                 "flag", "s_ready", "exp", "clamp", "fixed", "parts0", "pv", "pv_read", "o", "o_div", "o_read")
        s = {n: sem("xa_" + n) for n in names}
        S_BANK, M_BANK, PV_BANK, MISC = 0, 2, 6, 7
        block = life.enter_context(nc.Block())

        def wait(engine, semaphore, value):
            if not isinstance(value, int) or value > 0:
                engine.wait_ge(semaphore, value)

        def head(i, r):
            h = BUFS * i + r
            return h if not isinstance(h, int) or 0 <= h < NH else None

        def periods(engine, slot):
            def period(i, r):
                for jj in range(8):
                    slot(i, r, jj)
            for r in range(-1, 3):
                period(0, r)
            with engine.Fori(0, NH // BUFS - 1) as i:
                for r in range(3, 3 + BUFS):
                    period(i, r)
            for r in range(3, 6):
                period(NH // BUFS - 1, r)

        def stages(i, r, jj):
            return (i, r + 1, jj), (i, r - (jj < 3), (jj - 3) % 8), (i, r - 1 - (jj < 5), (jj - 5) % 8)

        @block.sync
        def _(sp):
            sp.dma_start(pick[:], a["pick"]).then_inc(s["pick"], 16)

            def load(i, b):
                h = BUFS * i + b
                wait(sp, s["s_ready"], 16 * (h - BUFS + 1))
                for g in range(6):
                    rows = slice(g * DH, g * DH + DH)
                    sp.dma_start(k_st[b][rows, :], k_parts[K_PART[g], h]).then_inc(s_kq[b], 16)
                    sp.dma_start(q_st[b][rows, :], q_parts[Q_PART[g], h]).then_inc(s_kq[b], 16)
                wait(sp, s["pv"], 8 * (h - BUFS + 1))
                sp.dma_start(v_st[b][:], v_heads.rearrange("b h p c w -> (b h) p (c w)")[h]).then_inc(s_vl[b], 16)

            for b in range(BUFS):
                load(0, b)
            with sp.Fori(1, NH // BUFS) as i:
                for b in range(BUFS):
                    load(i, b)

        @block.gpsimd
        def _(g):
            for n in range(BUFS):
                g.memset(k_st[n][PARTS:ROWS, :], 1.0).then_inc(s["const"], 1)
                g.wait_ge(s["const"], 2 * n + 1)
                g.memset(k_st[n][PARTS:PARTS + 1, :], 0.0).then_inc(s["const"], 1)

        @block.tensor
        def _(pe):
            def maxima(i, r, jj):
                h, b = head(i, r), r % BUFS
                if h is None:
                    return
                if jj == 0:
                    pe.wait_ge(s_kq[b], 16 * 12 * (i + r // BUFS + 1))
                wait(pe, s["m_read"], 8 * h + jj - 1)
                qc, kb = jj // 4, 2 * (jj % 4)
                for k in range(2):
                    mm = pe.matmul(psum[:, M_BANK + 2 * (jj % 2) + k, :], q_st[b][0:PARTS, qc * P:qc * P + P],
                                   k_st[b][0:PARTS, (kb + k) * 512:(kb + k + 1) * 512], start=True, stop=True)
                mm.then_inc(s["m_ready"], 1)

            def scores(i, r, jj):
                h, b = head(i, r), r % BUFS
                if h is None:
                    return
                if jj == 0:
                    pe.wait_ge(s["row"], h + 1)
                    pe.wait_ge(s["const"], 2 * BUFS)
                for j in (2 * jj, 2 * jj + 1):
                    wait(pe, s["exp"], 16 * h + j - 1)
                    for k in range(2):
                        c = 2 * j + k
                        mm = pe.matmul(psum[:, S_BANK + j % 2, k * T:k * T + T], k_st[b][:, c * P:c * P + P],
                                       q_st[b][:, :], start=True, stop=True)
                    mm.then_inc(s["s_ready"], 1)

            def values(i, r, jj):
                h, b = head(i, r), r % BUFS
                if h is None:
                    return
                if jj == 0:
                    pe.wait_ge(s["clamp"], h + 1)
                    pe.wait_ge(s_vl[b], 16 * (i + r // BUFS + 1))
                    pe.wait_ge(s["fixed"], 1)
                    wait(pe, s["pv_read"], h)
                for g in range(4):
                    c = 4 * jj + g
                    mm = pe.matmul(psum[32 * g:32 * g + VW, PV_BANK, 0:T], v_st[b][:, c * VW:c * VW + VW],
                                   probs[:, r % 2, c * T:c * T + T], start=(jj == 0), stop=(jj == 7))
                mm.then_inc(s["pv"], 1)

            def turn_maxima(i, r):
                h = head(i, r)
                if h is None:
                    return
                pe.wait_ge(s["parts"], h + 1)
                wait(pe, s["o_read"], h - 2)
                for qc in range(2):
                    mm = pe.matmul(psum[96:100, MISC, qc * P:qc * P + P], m_parts[:, qc, :], identb[:],
                                   start=True, stop=True)
                mm.then_inc(s["turned"], 1)

            def output(i, r):
                h = head(i, r)
                if h is None:
                    return
                pe.wait_ge(s["pv_read"], h + 1)
                wait(pe, s["o_read"], h)
                pe.wait_ge(s["row"], NH if isinstance(h, int) and h > NH - 3 else h + 3)
                for qc in range(2):
                    mm = pe.matmul(psum[:, MISC, 256 + qc * VW:256 + qc * VW + VW], pv_sb[:, qc * P:qc * P + P],
                                   pick[:], start=True, stop=True)
                mm.then_inc(s["o"], 1)

            def slot(i, r, jj):
                of_max, of_scores, of_values = stages(i, r, jj)
                maxima(*of_max)
                if jj == 6:
                    output(i, r - 2)
                if jj <= 4:
                    values(*of_values)
                scores(*of_scores)
                if jj > 4:
                    values(*of_values)
                if jj == 1:
                    turn_maxima(i, r)

            pe.wait_ge(s["pick"], 16)
            periods(pe, slot)

        @block.scalar
        def _(act):
            def exps(i, r, jj):
                h = head(i, r)
                if h is None:
                    return
                for j in (2 * jj, 2 * jj + 1):
                    act.wait_ge(s["s_ready"], 16 * h + j + 1)
                    if j % 2 == 0:
                        wait(act, s["pv"], 8 * (h - 2) + jj + 1)
                    act.activation(probs[:, r % 2, j * 512:j * 512 + 512], psum[:, S_BANK + j % 2, :],
                                   ACT.Exp).then_inc(s["exp"], 1)

            def slot(i, r, jj):
                _, of_scores, _ = stages(i, r, jj)
                h = head(i, r - 2)
                if jj == 4 and h is not None:
                    act.wait_ge(s["pv"], 8 * (h + 1))
                    wait(act, s["o"], h)
                    act.copy(pv_sb[:], psum[:, PV_BANK, 0:T]).then_inc(s["pv_read"], 1)
                h = head(i, r)
                if jj == 2 and h is not None:
                    act.wait_ge(s["turned"], h + 1)
                    wait(act, s["s_ready"], 16 * (h - 3))
                    act.copy(q_st[r % BUFS][PARTS:PARTS + 4, :], psum[96:100, MISC, 0:T]).then_inc(s["row"], 1)
                exps(*of_scores)

            periods(act, slot)

        @block.vector
        def _(v):
            v.memset(psum[:, PV_BANK, 0:T], 0.0).then_inc(s["fixed"], 1)
            flag_reg = life.enter_context(v.register("clip_flag"))

            def row_max(i, r, jj):
                h = head(i, r)
                if h is None:
                    return
                v.wait_ge(s["m_ready"], 8 * h + jj + 1)
                v.tensor_reduce(mx[:, r % 2, jj:jj + 1], psum[:, M_BANK + 2 * (jj % 2):M_BANK + 2 * (jj % 2) + 2, :],
                                AX.XY, ALU.max).then_inc(s["m_read"], 1)

            def chain(i, r, step):
                h = head(i, r)
                if h is None:
                    return
                inside, hi, mid, low = (m_parts[:, :, k] for k in range(4))
                if step == 0:
                    v.wait_ge(s["m_read"], 8 * h + 8)
                    v.tensor_reduce(raw_m[:], mx[:, r % 2, :].rearrange("p (q k) -> p q k", q=2), AX.X, ALU.max,
                                    negate=True).then_inc(s["raw"], 1)
                elif step == 1:
                    v.wait_ge(s["raw"], h + 1)
                    wait(v, s["turned"], h)
                    v.tensor_scalar(neg_m[:], raw_m[:], CLAMP - LOW, -CLAMP, ALU.min, ALU.max).then_inc(s["neg"], 1)
                    v.tensor_scalar(hi, raw_m[:], CLAMP - LOW, -CLAMP, ALU.min, ALU.max).then_inc(s["high"], 1)
                elif step == 2:
                    v.wait_ge(s["neg"], h + 1)
                    v.wait_ge(s["high"], h + 1)
                    v.tensor_tensor(m_rest[:], neg_m[:], hi, ALU.subtract).then_inc(s["rest"], 1)
                    v.tensor_tensor(inside, raw_m[:], neg_m[:], ALU.not_equal).then_inc(s["parts0"], 1)
                elif step == 3:
                    v.wait_ge(s["rest"], h + 1)
                    v.tensor_copy(mid, m_rest[:]).then_inc(s["mid"], 1)
                else:
                    v.wait_ge(s["mid"], h + 1)
                    v.wait_ge(s["parts0"], h + 1)
                    v.tensor_tensor(low, m_rest[:], mid, ALU.subtract).then_inc(s["parts"], 1)

            def read_flag(i, r):
                h = head(i, r)
                if h is None:
                    return
                v.wait_ge(s["row"], h + 1)
                v.tensor_reduce(flag[96:97, r % 2:r % 2 + 1], q_st[r % BUFS][96:97, :], AX.X, ALU.max).then_inc(s["flag"], 1)

            def clamp(i, r):
                h = head(i, r)
                if h is None:
                    return
                v.wait_ge(s["exp"], 16 * (h + 1))
                v.wait_ge(s["flag"], h + 1)
                v.memset(spare[:, r % 2:r % 2 + 1], 0.0)
                v.reg_load(flag_reg, flag[96:97, r % 2:r % 2 + 1])
                with v.If_ne(flag_reg, 0):
                    p = probs[:, r % 2, :]
                    v.tensor_scalar(p, p, 1.0, FLOOR, ALU.min, ALU.max).then_inc(s["clamp"], 1)
                with v.Else():
                    v.memset(spare[:, 2 + r % 2:3 + r % 2], 0.0).then_inc(s["clamp"], 1)

            def finish(i, r):
                h = head(i, r)
                if h is None:
                    return
                v.wait_ge(s["o"], h + 1)
                wait(v, s["o_read"], h)
                o = psum[:, MISC, 256:256 + 2 * VW].rearrange("p (q w) -> p q w", q=2)
                v.reciprocal(recip[:], o[:, :, DH]).then_inc(s["o_div"], 1)
                v.wait_ge(s["o_div"], h + 1)
                v.tensor_tensor(o_all[:, :, bass.ds(h * DH, DH)], o[:, :, 0:DH],
                                recip[:].unsqueeze(2).broadcast_to([P, 2, DH]), ALU.mult).then_inc(s["o_read"], 1)

            def slot(i, r, jj):
                of_max, _, _ = stages(i, r, jj)
                if jj == 0:
                    chain(i, r, 0)
                    chain(i, r, 1)
                row_max(*of_max)
                if jj == 0:
                    chain(i, r, 2)
                    chain(i, r, 3)
                    chain(i, r, 4)
                if jj == 3:
                    read_flag(i, r)
                    clamp(i, r - 1)
                if jj == 7:
                    finish(i, r - 2)

            periods(v, slot)


def attention_output(nc, which, w_dram, b_dram, psum, x_sb, ident, ones_row, o_all, oT):
    with ExitStack() as life:
        def sb(name, shape, dt):
            return life.enter_context(nc.sbuf_tensor(name, shape, dt))

        def sem(name):
            return life.enter_context(nc.semaphore(name))

        w = sb(which + "_wo", [P, FC, D], F32)
        b = sb(which + "_bo", [1, D], F32)
        s_load, s_turn, s_oT, s_y, s_x = (sem(which + n) for n in ("_load", "_turn", "_oT", "_y", "_x"))
        loads = 1 if b_dram is None else 2
        block = life.enter_context(nc.Block())

        @block.sync
        def _(sp):
            sp.dma_start(w[:], w_dram.rearrange("(c p) n -> p c n", p=P)).then_inc(s_load, 16)
            if b_dram is not None:
                sp.dma_start(b[:], b_dram).then_inc(s_load, 16)

        @block.tensor
        def _(pe):
            pe.wait_ge(s_load, 16 * loads)
            for n in range(4):
                for k in range(4):
                    t = 4 * (n % 2) + k
                    src = o_all[:, t % 2, (t // 2) * D + (n // 2) * P:(t // 2) * D + (n // 2) * P + P]
                    mm = pe.transpose(psum[:, n, k * P:k * P + P], src, ident[:])
                mm.then_inc(s_turn, 1)
            pe.wait_ge(s_oT, 4)
            for t in range(NT):
                bank = psum[:, 4 + t // 2, (t % 2) * D:(t % 2) * D + D]
                for c in range(FC):
                    mm = pe.matmul(bank, oT[:, c, t * P:t * P + P], w[:, c, :], start=(c == 0),
                                   stop=(b_dram is None and c == FC - 1))
                if b_dram is not None:
                    mm = pe.matmul(bank, ones_row[:], b[:], start=False, stop=True)
                if t % 2:
                    mm.then_inc(s_y, 1)

        @block.vector
        def _(v):
            for n in range(4):
                v.wait_ge(s_turn, n + 1)
                v.tensor_copy(oT[:, n // 2, (n % 2) * 512:(n % 2) * 512 + 512], psum[:, n, :]).then_inc(s_oT, 1)
            for m in range(NT // 2):
                v.wait_ge(s_y, m + 1)
                v.tensor_tensor(x_sb[:, 2 * m:2 * m + 2, :], x_sb[:, 2 * m:2 * m + 2, :],
                                psum[:, 4 + m, :].rearrange("p (t d) -> p t d", t=2), ALU.add).then_inc(s_x, 1)


def self_attention(nc, a, psum, x_sb, ident, neg_half, stats, mv, ve, rstd, xn, xnT, qk_rot, o_all):
    with ExitStack() as outer:
        v_all = outer.enter_context(nc.sbuf_tensor("v_all", [P, NT, D], F32))
        with ExitStack() as life:
            def sb(name, shape, dt):
                return life.enter_context(nc.sbuf_tensor(name, shape, dt))

            def sem(name):
                return life.enter_context(nc.semaphore(name))

            w = sb("w_qkv", [P, 5, FC, D], F32)
            cos = sb("cos", [P, 512], F32)
            sin = sb("sin", [P, 512], F32)
            direct = sb("direct", [P, 8, 512], F32)
            swapped = sb("swapped", [P, 8, 512], F32)
            s_load, s_turned, s_mm, s_read, s_add, s_vmm, s_v, s_store = (
                sem(n) for n in ("sp_load", "sp_turned", "sp_mm", "sp_read", "sp_add", "sp_vmm", "sp_v", "sp_store"))
            block = life.enter_context(nc.Block())
            norm_dve, norm_pool, norm_pe = norm_and_turn(
                nc, "ln2", psum, x_sb, ident, neg_half, stats, mv, ve, rstd, xn, xnT, lambda v: None, s_turned, sem)

            @block.sync
            def _(sp):
                for n, name in enumerate(("sq_w", "sk_w", "sq_sw", "sk_sw", "sv_w")):
                    sp.dma_start(w[:, n], a[name].rearrange("(c p) n -> p c n", p=P)).then_inc(s_load, 16)
                sp.dma_start(cos[:], a["cos"]).then_inc(s_load, 16)
                sp.dma_start(sin[:], a["sin"]).then_inc(s_load, 16)
                qk = qk_rot.rearrange("k (c h) d t -> k c (h d) t", c=FC)
                for n in range(8):
                    sp.wait_ge(s_add, n + 1)
                    sp.dma_start(qk[n // 4, (n // 2) % 2, :, (n % 2) * 512:(n % 2) * 512 + 512],
                                 direct[:, n, :]).then_inc(s_store, 16)
                sp.wait_ge(s_store, 16 * 8)

            @block.gpsimd
            def _(g):
                norm_pool(g)

            @block.tensor
            def _(pe):
                norm_pe(pe)
                pe.wait_ge(s_turned, 4)
                pe.wait_ge(s_load, 16 * 7)
                for n in range(8):
                    kind, fo, half = n // 4, (n // 2) % 2, n % 2
                    if n >= 4:
                        pe.wait_ge(s_read, 2 * (n - 4) + 2)
                    for sw in range(2):
                        for c in range(FC):
                            mm = pe.matmul(psum[:, 2 * (n % 4) + sw, :], w[:, 2 * sw + kind, c, fo * P:fo * P + P],
                                           xnT[:, c, half * 512:half * 512 + 512], start=(c == 0), stop=(c == FC - 1))
                    mm.then_inc(s_mm, 1)
                for t in range(NT):
                    if t % 2 == 0:
                        pe.wait_ge(s_read, 2 * (4 + t // 2) + 2)
                    for c in range(FC):
                        mm = pe.matmul(psum[:, t, 0:D], xnT[:, c, t * P:t * P + P], w[:, 4, c, :], start=(c == 0),
                                       stop=(c == FC - 1))
                    mm.then_inc(s_vmm, 1)

            @block.scalar
            def _(act):
                for t in range(NT):
                    act.wait_ge(s_vmm, t + 1)
                    act.copy(v_all[:, t, :], psum[:, t, 0:D]).then_inc(s_v, 1)

            @block.vector
            def _(v):
                norm_dve(v)
                v.wait_ge(s_load, 16 * 7)
                for n in range(8):
                    v.wait_ge(s_mm, n + 1)
                    v.tensor_tensor(direct[:, n, :], psum[:, 2 * (n % 4), :], cos[:], ALU.mult).then_inc(s_read, 1)
                    v.tensor_tensor(swapped[:, n, :], psum[:, 2 * (n % 4) + 1, :], sin[:], ALU.mult).then_inc(s_read, 1)
                    v.wait_ge(s_read, 2 * n + 2)
                    v.tensor_tensor(direct[:, n, :], direct[:, n, :], swapped[:, n, :], ALU.add).then_inc(s_add, 1)

        with ExitStack() as life:
            def sb(name, shape, dt):
                return life.enter_context(nc.sbuf_tensor(name, shape, dt))

            def sem(name):
                return life.enter_context(nc.semaphore(name))

            qk = [sb(f"qk{s}", [DH, 2, T], F32) for s in range(4)]
            vh = [sb(f"vh{s}", [P, 2, DH], F32) for s in range(4)]
            mask = sb("mask", [P, 2 * T], F32)
            masked = sb("masked", [P, 2, 2 * T], F32)
            probs = sb("sprobs", [P, 2, 2, T], F32)
            probsT = sb("probsT", [P, 2, 3, P], F32)
            neg_m = sb("sneg_m", [P, 2, 2], F32)
            total = sb("total", [P, 2, 2], F32)
            recip = sb("srecip", [P, 2], F32)
            total_max = sb("total_max", [P, 2, 2], F32)
            s_raw = sem("sa_raw")
            s_mask = sem("sa_mask")
            s_load = [sem(f"sa_load{s}") for s in range(4)]
            s = {n: sem("sa_" + n) for n in ("s", "masked", "max", "exp", "turn", "pT", "o", "o_div", "o_read")}
            block = life.enter_context(nc.Block())

            @block.sync
            def _(sp):
                sp.dma_start(mask[:], a["mask"]).then_inc(s_mask, 16)

                def load(h, slot):
                    for k in range(2):
                        sp.dma_start(qk[slot][:, k, :], qk_rot[k, h % H, :, bass.ds((h // H) * T, T)]
                                     ).then_inc(s_load[slot], 16)
                    src = v_all[:, bass.ds((h // H) * 2, 2), bass.ds((h % H) * DH, DH)]
                    sp.dma_start(vh[slot][:], src).then_inc(s_load[slot], 16)

                for h in range(4):
                    load(h, h)
                with sp.Fori(1, NH // 4) as i:
                    for r in range(4):
                        sp.wait_ge(s["o"], 4 * i + r - 3)
                        load(4 * i + r, r)

            def periods(engine, step):
                for h in range(4):
                    step(0, h)
                with engine.Fori(1, NH // 4) as i:
                    for r in range(4):
                        step(i, r)
                for r in range(2):
                    step(NH // 4, r)

            def on(i, r, lag):
                h = 4 * i + r - lag
                return h, not isinstance(i, int) or 0 <= h < NH, not isinstance(i, int)

            @block.tensor
            def _(pe):
                def step(i, r):
                    h, live, loop = on(i, r, 0)
                    if live:
                        pe.wait_ge(s_load[r], 48 * (i + 1))
                        if loop or h >= 2:
                            pe.wait_ge(s["masked"], h - 1)
                        for qc in range(2):
                            mm = pe.matmul(psum[:, r % 2, qc * T:qc * T + T], qk[r][:, 0, qc * P:qc * P + P],
                                           qk[r][:, 1, :], start=True, stop=True)
                        mm.then_inc(s["s"], 1)
                    h, live, loop = on(i, r, 1)
                    if live:
                        par = (r - 1) % 2
                        pe.wait_ge(s["exp"], h + 1)
                        if loop or h >= 2:
                            pe.wait_ge(s["pT"], h - 1)
                        for k, (qc, kc) in enumerate(((0, 0), (1, 0), (1, 1))):
                            mm = pe.transpose(psum[:, 2 + par, k * P:k * P + P], probs[:, par, qc, kc * P:kc * P + P],
                                              ident[:])
                        mm.then_inc(s["turn"], 1)
                    h, live, loop = on(i, r, 2)
                    if live:
                        par, slot = r % 2, (r - 2) % 4
                        pe.wait_ge(s["pT"], h + 1)
                        if loop or h >= 2:
                            pe.wait_ge(s["o_read"], h - 1)
                        bank = psum[:, 4 + par, :]
                        pe.matmul(bank[:, 0:DH], probsT[:, par, 0, :], vh[slot][:, 0, :], start=True, stop=True)
                        pe.matmul(bank[:, DH:2 * DH], probsT[:, par, 1, :], vh[slot][:, 0, :], start=True, stop=False)
                        pe.matmul(bank[:, DH:2 * DH], probsT[:, par, 2, :], vh[slot][:, 1, :], start=False,
                                  stop=True).then_inc(s["o"], 1)

                periods(pe, step)

            @block.scalar
            def _(act):
                def step(i, r):
                    h, live, loop = on(i, r, 0)
                    if live:
                        act.wait_ge(s["max"], h + 1)
                        if loop or h >= 2:
                            act.wait_ge(s["turn"], h - 1)
                            act.wait_ge(s["o_div"], h - 1)
                        for qc in range(2):
                            last = act.activation(probs[:, r % 2, qc, :], masked[:, r % 2, qc * T:qc * T + T], ACT.Exp,
                                                  bias=neg_m[:, r % 2, qc:qc + 1], scale=SCALE,
                                                  accum_out=total[:, r % 2, qc:qc + 1])
                        last.then_inc(s["exp"], 1)
                    h, live, loop = on(i, r, 1)
                    if live:
                        par = (r - 1) % 2
                        act.wait_ge(s["turn"], h + 1)
                        if loop or h >= 2:
                            act.wait_ge(s["o"], h - 1)
                        act.copy(probsT[:, par].rearrange("p k q -> p (k q)"), psum[:, 2 + par, 0:3 * P]).then_inc(s["pT"], 1)

                periods(act, step)

            @block.vector
            def _(v):
                v.wait_ge(s_mask, 16)

                def step(i, r):
                    h, live, loop = on(i, r, 0)
                    if live:
                        v.wait_ge(s["s"], h + 1)
                        if loop or h >= 2:
                            v.wait_ge(s["exp"], h - 1)
                        v.tensor_tensor(masked[:, r % 2, :], psum[:, r % 2, :], mask[:], ALU.min).then_inc(s["masked"], 1)
                        v.wait_ge(s["masked"], h + 1)
                        v.tensor_reduce(total_max[:, r % 2, :], masked[:, r % 2, :].rearrange("p (q k) -> p q k", q=2),
                                        AX.X, ALU.max).then_inc(s_raw, 1)
                        v.wait_ge(s_raw, h + 1)
                        v.tensor_scalar(neg_m[:, r % 2, :], total_max[:, r % 2, :], -SCALE, None,
                                        ALU.mult).then_inc(s["max"], 1)
                    h, live, loop = on(i, r, 2)
                    if live:
                        par = r % 2
                        v.wait_ge(s["o"], h + 1)
                        if loop or h >= 1:
                            v.wait_ge(s["o_read"], h)
                        v.reciprocal(recip[:], total[:, par, :]).then_inc(s["o_div"], 1)
                        v.wait_ge(s["o_div"], h + 1)
                        o = psum[:, 4 + par, 0:2 * DH].rearrange("p (q d) -> p q d", q=2)
                        v.tensor_tensor(o_all[:, :, bass.ds(h * DH, DH)], o,
                                        recip[:].unsqueeze(2).broadcast_to([P, 2, DH]), ALU.mult).then_inc(s["o_read"], 1)

                periods(v, step)


def experts(nc, a, psum, x_sb, ident, ones_row, neg_half, stats, mv, ve, rstd, xn, xnT, out):
    with ExitStack() as life:
        def sb(name, shape, dt):
            return life.enter_context(nc.sbuf_tensor(name, shape, dt))

        def sem(name):
            return life.enter_context(nc.semaphore(name))

        wr = sb("wr", [P, FC, E], F32)
        br = sb("br", [1, E], F32)
        b1 = sb("b1", [P, E, HC], F32)
        b2 = sb("b2", [E, D], F32)
        w1 = [sb(f"w1_{p}", [P, FC, HID], F32) for p in range(2)]
        w2 = [sb(f"w2_{p}", [P, HC, D], F32) for p in range(2)]
        hid = sb("hid", [P, HC, TOK], F32)
        logits = sb("logits", [P, NT, E], F32)
        top = sb("top", [P, NT, 8], F32)
        shifted = sb("shifted", [P, NT, E], F32)
        gate = sb("gate", [P, NT, E], F32)
        gates = sb("gates", [P, NT, E], F32)
        gsum = sb("gsum", [P, NT], F32)
        grec = sb("grec", [P, NT], F32)
        gatesT = sb("gatesT", [E, TOK], F32)
        acc = sb("acc", [P, NT, D], F32)
        b1_cur = sb("b1_cur", [P, 2, HC], F32)
        gate_cur = sb("gate_cur", [P, 2, NT], F32)
        s_b1, s_acc0b, s_gc = sem("ex_b1"), sem("ex_rec"), sem("ex_gate")
        s_load, s_turned, s_log, s_g, s_gexp, s_gT, s_gTc, s_b2, s_acc0 = (
            sem(n) for n in ("ex_load", "ex_turned", "ex_log", "ex_g", "ex_gexp", "ex_gT", "ex_gTc", "ex_b2", "ex_acc0"))
        s_w = [sem(f"ex_w{p}") for p in range(2)]
        s_up, s_gelu, s_down, s_acc, s_out = (sem(n) for n in ("ex_up", "ex_gelu", "ex_down", "ex_acc", "ex_out"))
        block = life.enter_context(nc.Block())
        norm_dve, norm_pool, norm_pe = norm_and_turn(
            nc, "ln3", psum, x_sb, ident, neg_half, stats, mv, ve, rstd, xn, xnT, lambda v: None, s_turned, sem)

        def load(sp, e, p):
            sp.dma_start(w1[p][:], a["e1_w"][e].rearrange("(c p) n -> p c n", p=P)).then_inc(s_w[p], 16)
            sp.dma_start(w2[p][:], a["e2_w"][e].rearrange("(c p) n -> p c n", p=P)).then_inc(s_w[p], 16)

        @block.sync
        def _(sp):
            sp.dma_start(wr[:], a["r_w"].rearrange("(c p) n -> p c n", p=P)).then_inc(s_load, 16)
            sp.dma_start(br[:], a["r_b"]).then_inc(s_load, 16)
            sp.dma_start(b1[:], a["e1_b"]).then_inc(s_load, 16)
            sp.dma_start(b2[:], a["e2_b"]).then_inc(s_load, 16)
            load(sp, 0, 0)
            load(sp, 1, 1)
            with sp.Fori(1, E // 2) as i:
                for p in range(2):
                    sp.wait_ge(s_down, NT * (2 * i + p - 1))
                    load(sp, 2 * i + p, p)
            sp.wait_ge(s_acc, NT * E)
            sp.dma_start(out.rearrange("(t p) d -> p t d", p=P), acc[:]).then_inc(s_out, 16)
            sp.wait_ge(s_out, 16)

        @block.gpsimd
        def _(g):
            norm_pool(g)

        @block.tensor
        def _(pe):
            norm_pe(pe)
            pe.wait_ge(s_turned, 4)
            pe.wait_ge(s_load, 64)
            for t in range(NT):
                bank = psum[:, 4, t * E:t * E + E]
                for c in range(FC):
                    pe.matmul(bank, xnT[:, c, t * P:t * P + P], wr[:, c, :], start=(c == 0), stop=False)
                mm = pe.matmul(bank, ones_row[:], br[:], start=False, stop=True)
            mm.then_inc(s_log, 1)
            pe.wait_ge(s_g, 7)
            for t in range(NT):
                mm = pe.transpose(psum[0:E, 5 + t // 4, (t % 4) * P:(t % 4) * P + P], gates[:, t, :], ident[:])
            mm.then_inc(s_gT, 1)
            pe.wait_ge(s_gTc, 1)
            for t in range(NT):
                mm = pe.matmul(psum[:, t // 2, (t % 2) * D:(t % 2) * D + D], gatesT[:, t * P:t * P + P], b2[:],
                               start=True, stop=True)
            mm.then_inc(s_b2, 1)
            pe.wait_ge(s_acc0, 1)

            def expert(i, p, first):
                e = 2 * i + p
                pe.wait_ge(s_w[p], 32 * (i + 1))
                for n in range(2 * HC):
                    if n >= 4:
                        pe.wait_ge(s_gelu, 2 * HC * e + n - 3)
                    elif not first:
                        pe.wait_ge(s_gelu, 2 * HC * e + n - 3)
                    for c in range(FC):
                        mm = pe.matmul(psum[:, n % 4, :], w1[p][:, c, (n // 2) * P:(n // 2) * P + P],
                                       xnT[:, c, (n % 2) * 512:(n % 2) * 512 + 512], start=(c == 0), stop=(c == FC - 1))
                    mm.then_inc(s_up, 1)
                pe.wait_ge(s_gelu, 2 * HC * (e + 1))
                for t in range(NT):
                    if t >= 4 or not first:
                        pe.wait_ge(s_acc, NT * e + t - 3)
                    for c in range(HC):
                        mm = pe.matmul(psum[:, 4 + t % 4, 0:D], hid[:, c, t * P:t * P + P], w2[p][:, c, :],
                                       start=(c == 0), stop=(c == HC - 1))
                    mm.then_inc(s_down, 1)

            expert(0, 0, True)
            expert(0, 1, False)
            with pe.Fori(1, E // 2) as i:
                for p in range(2):
                    expert(i, p, False)

        @block.scalar
        def _(act):
            act.wait_ge(s_g, 4)
            act.activation(gate[:], shifted[:], ACT.Exp).then_inc(s_gexp, 1)

            def expert(i, p, first):
                e = 2 * i + p
                for n in range(2 * HC):
                    act.wait_ge(s_up, 2 * HC * e + n + 1)
                    if n == 0 and not first:
                        act.wait_ge(s_down, NT * e)
                    act.activation(hid[:, n // 2, (n % 2) * 512:(n % 2) * 512 + 512], psum[:, n % 4, :], ACT.Gelu,
                                   bias=b1_cur[:, p, n // 2:n // 2 + 1]).then_inc(s_gelu, 1)

            def bias(i, p, first):
                if not first:
                    act.wait_ge(s_gelu, 2 * HC * (2 * i + p))
                act.copy(b1_cur[:, p, :], b1[:, 2 * i + p, :]).then_inc(s_b1, 1)
                act.wait_ge(s_b1, 2 * i + p + 1)

            act.wait_ge(s_load, 64)
            for p in range(2):
                bias(0, p, p == 0)
                expert(0, p, p == 0)
            with act.Fori(1, E // 2) as i:
                for p in range(2):
                    bias(i, p, False)
                    expert(i, p, False)

        @block.vector
        def _(v):
            norm_dve(v)
            v.wait_ge(s_log, 1)
            v.tensor_copy(logits[:], psum[:, 4, 0:NT * E].rearrange("p (t e) -> p t e", t=NT)).then_inc(s_g, 1)
            v.wait_ge(s_g, 1)
            for t in range(NT):
                last = v.max(top[:, t, :], logits[:, t, :])
            last.then_inc(s_g, 1)
            v.wait_ge(s_g, 2)
            v.tensor_tensor(gates[:], logits[:], top[:, :, 1:2].broadcast_to([P, NT, E]), ALU.is_ge).then_inc(s_g, 1)
            v.tensor_tensor(shifted[:], logits[:], top[:, :, 0:1].broadcast_to([P, NT, E]),
                            ALU.subtract).then_inc(s_g, 1)
            v.wait_ge(s_gexp, 1)
            v.wait_ge(s_g, 4)
            v.tensor_tensor(gate[:], gate[:], gates[:], ALU.mult).then_inc(s_g, 1)
            v.wait_ge(s_g, 5)
            v.tensor_reduce(gsum[:], gate[:], AX.X, ALU.add).then_inc(s_g, 1)
            v.wait_ge(s_g, 6)
            v.reciprocal(grec[:], gsum[:]).then_inc(s_acc0b, 1)
            v.wait_ge(s_acc0b, 1)
            v.tensor_tensor(gates[:], gate[:], grec[:].unsqueeze(2).broadcast_to([P, NT, E]), ALU.mult).then_inc(s_g, 1)
            v.wait_ge(s_gT, 1)
            v.tensor_copy(gatesT[:].rearrange("e (a t) -> e a t", a=2), psum[0:E, 5:7, :]).then_inc(s_gTc, 1)
            v.wait_ge(s_b2, 1)
            v.wait_ge(s_g, 7)
            v.tensor_tensor(acc[:], x_sb[:], psum[:, 0:4, :].rearrange("p a (t d) -> p (a t) d", t=2),
                            ALU.add).then_inc(s_acc0, 1)
            v.wait_ge(s_acc0, 1)

            def expert(i, p):
                e = 2 * i + p
                v.tensor_copy(gate_cur[:, p, :], gates[:, :, bass.ds(e, 1)].rearrange("p t o -> p (t o)")).then_inc(s_gc, 1)
                v.wait_ge(s_gc, e + 1)
                for t in range(NT):
                    v.wait_ge(s_down, NT * e + t + 1)
                    v.scalar_tensor_tensor(out=acc[:, t, :], in0=psum[:, 4 + t % 4, 0:D], scalar=gate_cur[:, p, t:t + 1],
                                           in1=acc[:, t, :], op0=ALU.mult, op1=ALU.add).then_inc(s_acc, 1)

            expert(0, 0)
            expert(0, 1)
            with v.Fori(1, E // 2) as i:
                for p in range(2):
                    expert(i, p)


def constants():
    inv = 1.0 / np.float32(10000.0) ** (np.arange(0, DH, 2, dtype=np.float32) / DH)
    ang = np.arange(T, dtype=np.float32)[:, None] * inv[None, :].astype(np.float32)
    cos = np.concatenate([np.cos(ang), np.cos(ang)], -1).T
    sin = np.concatenate([-np.sin(ang), np.sin(ang)], -1).T
    big = np.float32(3e38)
    mask = np.full((P, 2, T), big, np.float32)
    for qc in range(2):
        mask[:, qc][np.arange(T)[None, :] > (qc * P + np.arange(P))[:, None]] = -big
    pick = np.zeros((P, VW), np.float32)
    for g in range(4):
        pick[32 * g + np.arange(VW), np.arange(VW)] = 1.0
    return {
        "ident": np.eye(P, dtype=np.float32), "pick": pick, "mask": mask.reshape(P, 2 * T),
        "cos": np.tile(cos, (P // DH, 2)).astype(np.float32), "sin": np.tile(sin, (P // DH, 2)).astype(np.float32),
    }


def kernel(x, ctx_768, L0_xattn_Wq, L0_xattn_bq, L0_xattn_Wk, L0_xattn_bk, L0_xattn_Wv, L0_xattn_bv, L0_xattn_Wo,
           L0_xattn_bo, L0_attn_Wq, L0_attn_Wk, L0_attn_Wv, L0_attn_Wo, L0_ffn_W1, L0_ffn_b1, L0_ffn_W2, L0_ffn_b2,
           L0_ffn_Wr, L0_ffn_br):
    import concourse.bacc as _bacc
    from concourse.bass_utils import run_bass_kernel_spmd as _run

    def swap(w):
        return np.asarray(w).reshape(H, 2, DH // 2, D)[:, ::-1].reshape(D, D)

    arrays = {
        "x": np.asarray(x).reshape(TOK, D), "ctxT": np.asarray(ctx_768).transpose(0, 2, 1),
        "xq_w": L0_xattn_Wq, "xq_b": np.asarray(L0_xattn_bq).reshape(FC, P).T, "xk_w": L0_xattn_Wk,
        "xk_b": np.asarray(L0_xattn_bk).reshape(1, D), "xv_w": L0_xattn_Wv, "xv_b": np.asarray(L0_xattn_bv).reshape(1, D),
        "xo_w": L0_xattn_Wo, "xo_b": np.asarray(L0_xattn_bo).reshape(1, D),
        "sq_w": np.asarray(L0_attn_Wq).T, "sk_w": np.asarray(L0_attn_Wk).T, "sq_sw": swap(L0_attn_Wq).T,
        "sk_sw": swap(L0_attn_Wk).T, "sv_w": np.asarray(L0_attn_Wv).T, "so_w": np.asarray(L0_attn_Wo).T,
        "r_w": L0_ffn_Wr, "r_b": np.asarray(L0_ffn_br).reshape(1, E), "e1_w": L0_ffn_W1,
        "e1_b": np.asarray(L0_ffn_b1).reshape(E, HC, P).transpose(2, 0, 1), "e2_w": L0_ffn_W2, "e2_b": L0_ffn_b2,
        **constants(),
    }
    arrays = {name: np.ascontiguousarray(v) for name, v in arrays.items()}
    nc = _bacc.Bacc("TRN2", target_bir_lowering=False, num_devices=1)
    args = {name: nc.dram_tensor("in_" + name, v.shape, mybir.dt.from_np(v.dtype), kind="ExternalInput").ap()
            for name, v in arrays.items()}
    out = nc.dram_tensor("out", (TOK, D), F32, kind="ExternalOutput").ap()
    build_program(nc, args, out)
    r = _run(nc, [{"in_" + name: v for name, v in arrays.items()}], core_ids=[0])
    return r.results[0]["out"].reshape(B, T, D)
```

```python
from contextlib import ExitStack

import numpy as np

import concourse.bass as bass
from concourse import mybir

F32 = mybir.dt.float32
F32R = mybir.dt.float32r
BF16 = mybir.dt.bfloat16
ALU = mybir.AluOpType
ACT = mybir.ActivationFunctionType
AX = mybir.AxisListType

P = 128
B, T, D = 4, 256, 256
S, DC = 4096, 192
H = 16
DH = D // H
NH = B * H
TOK = B * T
NT = TOK // P
FC = D // P
E, HID = 8, 1024
HC = HID // P
KB = 512
NBLK = B * S // KB
NC = S // P
VW = DH + 1
PARTS = 6 * DH
PAIRS = ((0, 0), (0, 1), (1, 0))
K_PART = (0, 0, 0, 1, 1, 2)
Q_PART = (0, 1, 2, 0, 1, 0)
SCALE = DH ** -0.5
CLAMP = 10000.0
EPS = 1e-5
LOW = 64.0
FLOOR = float(np.exp(-LOW))


def wait(engine, semaphore, value):
    if not isinstance(value, int) or value > 0:
        engine.wait_ge(semaphore, value)


def tile_statistics(v, x, stats, tiles, s_stat):
    for t in tiles:
        v.bn_stats(stats[:, t, :], x[:, t, :]).then_inc(s_stat, 1)


def row_variances(v, stats, mv, ve, s_stat):
    v.wait_ge(s_stat, NT)
    for t in range(NT):
        last = v.bn_aggr(mv[:, t, :], stats[:, t, :])
    last.then_inc(s_stat, 1)
    v.wait_ge(s_stat, NT + 1)
    v.tensor_scalar(ve[:], mv[:, :, 1], EPS, None, ALU.add).then_inc(s_stat, 1)


def row_scales(g, ve, neg_half, rstd, s_stat, s_rstd):
    g.wait_ge(s_stat, NT + 2)
    g.tensor_tensor(rstd[:], ve[:], neg_half[:], ALU.pow).then_inc(s_rstd, 1)


def build_program(nc, a, out):
    with ExitStack() as life:
        def dram(name, shape, dt):
            return nc.dram_tensor(name, shape, dt).ap()

        def sem(name):
            return life.enter_context(nc.semaphore(name))

        psum = life.enter_context(nc.psum_tensor("psum", [P, 8, 512], F32))
        x_sb = life.enter_context(nc.sbuf_tensor("x_sb", [P, NT, D], F32))
        ident = life.enter_context(nc.sbuf_tensor("ident", [P, P], F32))
        identb = life.enter_context(nc.sbuf_tensor("identb", [P, P], BF16))
        ones_row = life.enter_context(nc.sbuf_tensor("ones_row", [1, P], F32))
        neg_half = life.enter_context(nc.sbuf_tensor("neg_half", [P, NT], F32))
        stats = life.enter_context(nc.sbuf_tensor("stats", [P, NT, 6], F32))
        mv = life.enter_context(nc.sbuf_tensor("mv", [P, NT, 2], F32))
        ve = life.enter_context(nc.sbuf_tensor("ve", [P, NT], F32))
        rstd = life.enter_context(nc.sbuf_tensor("rstd", [P, NT], F32))
        o_all = life.enter_context(nc.sbuf_tensor("o_all", [P, FC, NH * DH], F32))
        xn = life.enter_context(nc.sbuf_tensor("xn", [P, NT, D], F32))
        xnT = life.enter_context(nc.sbuf_tensor("xnT", [P, FC, TOK], F32))

        wo = life.enter_context(nc.sbuf_tensor("wo", [P, 2, FC, D], F32))
        bo = life.enter_context(nc.sbuf_tensor("bo", [1, D], F32))
        s_wo = sem("wo_load")

        k_parts = dram("k_parts", (3, NH, DH, S), BF16)
        q_parts = dram("q_parts", (3, NH, DH, T), BF16)
        v_heads = dram("v_heads", (B, H, P, NC, VW), F32)
        qk_stacked = dram("qk_stacked", (2, H, PARTS, TOK), BF16)

        project_inputs(nc, a, psum, x_sb, ident, identb, ones_row, neg_half, stats, mv, ve, rstd, xn, xnT, q_parts,
                       k_parts, v_heads)
        cross_attention(nc, a, psum, identb, k_parts, q_parts, v_heads, o_all, wo, bo, s_wo)
        norm_scratch = (neg_half, stats, mv, ve, rstd)
        attention_output(nc, "cross", wo[:, 0], bo, s_wo, 3, psum, x_sb, ident, ones_row, o_all, xnT, *norm_scratch)
        self_attention(nc, a, psum, x_sb, ident, identb, mv, rstd, xn, xnT, qk_stacked, o_all)
        attention_output(nc, "self", wo[:, 1], None, s_wo, 3, psum, x_sb, ident, ones_row, o_all, xnT, *norm_scratch)
        experts(nc, a, psum, x_sb, ident, ones_row, mv, rstd, xn, xnT, out)


def norm_and_turn(which, psum, x, ident, mv, rstd, xn, xnT, done_sem, sem):
    s_xn, s_turn = (sem(which + n) for n in ("_xn", "_turn"))

    def dve(v):
        for t in range(NT):
            v.tensor_scalar(xn[:, t, :], x[:, t, :], mv[:, t, 0:1], rstd[:, t:t + 1], ALU.subtract,
                            ALU.mult).then_inc(s_xn, 1)
        for n in range(4):
            v.wait_ge(s_turn, n + 1)
            v.tensor_copy(xnT[:, n // 2, (n % 2) * 512:(n % 2) * 512 + 512], psum[:, n, :]).then_inc(done_sem, 1)

    def pe(t_):
        for n in range(4):
            for k in range(4):
                t = 4 * (n % 2) + k
                t_.wait_ge(s_xn, t + 1)
                mm = t_.transpose(psum[:, n, k * P:k * P + P], xn[:, t, (n // 2) * P:(n // 2) * P + P], ident[:])
            mm.then_inc(s_turn, 1)

    return dve, pe


def project_queries(nc, life, a, psum, x_sb, ident, identb, ones_row, neg_half, stats, mv, ve, rstd, xn, xnT, q_parts):
    def sb(name, shape, dt):
        return life.enter_context(nc.sbuf_tensor(name, shape, dt))

    def sem(name):
        return life.enter_context(nc.semaphore(name))

    wq = sb("wq", [P, FC, D], F32)
    bq = sb("bq", [P, FC], F32)
    q_full = sb("q_full", [P, 4, 512], F32)
    rest = sb("rest", [P, 4, 512], F32)
    parts = sb("parts", [P, 3, 4, 512], BF16)
    s_load, s_const, s_turned, s_q, s_full = (sem(n) for n in ("pq_load", "pq_const", "pq_turned", "pq_q", "pq_full"))
    s_hi, s_rest, s_mid, s_low, s_store = (sem(n) for n in ("pq_hi", "pq_rest", "pq_mid", "pq_low", "pq_store"))
    s_stat, s_rstd = sem("ln1_stat"), sem("ln1_rstd")
    norm_dve, norm_pe = norm_and_turn("ln1", psum, x_sb, ident, mv, rstd, xn, xnT, s_turned, sem)

    def load(sp):
        sp.dma_start(x_sb[:], a["x"].rearrange("(t p) d -> p t d", p=P)).then_inc(s_load, 16)
        sp.dma_start(ident[:], a["ident"]).then_inc(s_load, 16)
        sp.dma_start(wq[:], a["xq_w"].rearrange("(c p) n -> p c n", p=P)).then_inc(s_load, 16)
        sp.dma_start(bq[:], a["xq_b"]).then_inc(s_load, 16)

    def store(sp):
        sp.wait_ge(s_hi, 4)
        sp.wait_ge(s_low, 8)
        for part in range(3):
            for c in range(FC):
                dst = q_parts[part].rearrange("(b c h) d t -> c (h d) b t", b=B, c=FC)[c]
                src = parts[:, part, 2 * c:2 * c + 2, :].rearrange("p m (b t) -> p (m b) t", b=2)
                sp.dma_start(dst, src).then_inc(s_store, 16)

    def constants_and_norm(g):
        g.memset(neg_half[:], -0.5).then_inc(s_const, 1)
        g.memset(ones_row[:], 1.0)
        g.wait_ge(s_const, 1)
        row_scales(g, ve, neg_half, rstd, s_stat, s_rstd)

    def products(pe):
        norm_pe(pe)
        pe.wait_ge(s_turned, 4)
        for n in range(4):
            for c in range(FC):
                mm = pe.matmul(psum[:, 4 + n, :], wq[:, c, (n // 2) * P:(n // 2) * P + P],
                               xnT[:, c, (n % 2) * 512:(n % 2) * 512 + 512], start=(c == 0), stop=(c == FC - 1))
            mm.then_inc(s_q, 1)

    def high_and_middle(act):
        for n in range(4):
            act.wait_ge(s_full, n + 1)
            act.copy(parts[:, 0, n, :], q_full[:, n, :]).then_inc(s_hi, 1)
        for n in range(4):
            act.wait_ge(s_rest, n + 1)
            act.copy(parts[:, 1, n, :], rest[:, n, :]).then_inc(s_mid, 1)

    def norm(v):
        v.wait_ge(s_load, 16 * 4)
        tile_statistics(v, x_sb, stats, range(NT), s_stat)
        row_variances(v, stats, mv, ve, s_stat)
        v.wait_ge(s_rstd, 1)
        norm_dve(v)
        v.tensor_copy(identb[:], ident[:])

    def full(v):
        for n in range(4):
            v.wait_ge(s_q, n + 1)
            v.tensor_scalar(q_full[:, n, :], psum[:, 4 + n, :], bq[:, n // 2:n // 2 + 1], SCALE, ALU.add,
                            ALU.mult).then_inc(s_full, 1)

    def rest_and_low(v):
        for n in range(4):
            v.wait_ge(s_hi, n + 1)
            v.tensor_tensor(rest[:, n, :], q_full[:, n, :], parts[:, 0, n, :], ALU.subtract).then_inc(s_rest, 1)
        for n in range(4):
            v.wait_ge(s_mid, n + 1)
            v.tensor_tensor(parts[:, 2, n, :], rest[:, n, :], parts[:, 1, n, :], ALU.subtract).then_inc(s_low, 2)

    steps = dict(load=load, store=store, constants_and_norm=constants_and_norm, products=products,
                 high_and_middle=high_and_middle, norm=norm, full=full, rest_and_low=rest_and_low)
    return steps, s_full, s_store


def project_inputs(nc, a, psum, x_sb, ident, identb, ones_row, neg_half, stats, mv, ve, rstd, xn, xnT, q_parts, k_parts,
                   v_heads):
    with ExitStack() as life:
        def sb(name, shape, dt):
            return life.enter_context(nc.sbuf_tensor(name, shape, dt))

        def sem(name):
            return life.enter_context(nc.semaphore(name))

        R2 = DC - P
        w_a = sb("w_a", [P, 2, D], F32)
        w_b = sb("w_b", [P, 2, D], F32)
        bias = sb("kv_bias", [R2 + 2, 2, D], F32)
        bias_hi = sb("kv_bias_hi", [R2 + 2, 2, D], F32R)
        w_hi = sb("w_hi", [P, 2, D], F32R)
        w_lo = sb("w_lo", [P, 2, D], F32R)
        w_both = sb("w_both", [P, 2, D], F32R)
        w_last = sb("w_last", [R2 + 2, 2, D], F32R)
        ctx_a = sb("ctx_a", [P, 4, KB], F32)
        ctx_b = sb("ctx_b", [R2, 4, KB], F32)
        x_hi = sb("x_hi", [P, 2, KB], F32R)
        x_lo = sb("x_lo", [P, 2, KB], F32R)
        x_both = sb("x_both", [P, 2, KB], F32R)
        x_last = sb("x_last", [R2 + 2, 2, KB], F32R)
        ones = sb("kv_ones", [R2 + 2, 2, KB], F32)
        parts = sb("kparts", [P, 2, 3, FC, KB], BF16)
        rest = sb("krest", [P, 2, FC, KB], F32)
        vals = sb("vals", [P, 2, H, 8, VW], F32)
        s_w, s_ones, s_wh, s_wp, s_lead, s_lo = (sem("pc_" + n) for n in ("w", "ones", "wh", "wp", "lead", "lo"))
        s_ctx = [sem(f"pc_ctx{r}") for r in range(4)]
        s_k, s_v, s_hi, s_rest, s_mid, s_low, s_vals = (
            sem("pc_" + n) for n in ("k", "v", "hi", "rest", "mid", "low", "vals"))
        s_store = [sem(f"pc_store{p}") for p in range(2)]
        s_vstore = [sem(f"pc_vstore{p}") for p in range(2)]
        queries, s_qfull, s_qstore = project_queries(nc, life, a, psum, x_sb, ident, identb, ones_row, neg_half, stats,
                                                     mv, ve, rstd, xn, xnT, q_parts)
        block = life.enter_context(nc.Block())

        def each_block(engine, work):
            for r in range(4):
                work(0, r)
            with engine.Fori(1, NBLK // 4) as i:
                for r in range(4):
                    work(i, r)

        def load(sp, i, r):
            n = 4 * i + r
            cols = bass.ds((n % 8) * KB, KB)
            sp.dma_start(ctx_a[:, r, :], a["ctxT"][n // 8, 0:P, cols]).then_inc(s_ctx[r], 16)
            sp.dma_start(ctx_b[:, r, :], a["ctxT"][n // 8, P:DC, cols]).then_inc(s_ctx[r], 16)

        def store(sp, i, r):
            n, p, m = 4 * i + r, r % 2, 2 * i + r // 2
            sp.wait_ge(s_hi, 2 * (n + 1))
            sp.wait_ge(s_mid, 2 * (n + 1))
            sp.wait_ge(s_low, 2 * (n + 1))
            kd = k_parts.rearrange("s (b c h) d t -> b (h d) s c t", b=B, c=FC)
            for c in range(FC):
                sp.dma_start(kd[n // 8, :, :, c, bass.ds((n % 8) * KB, KB)], parts[:, p, :, c, :]).then_inc(s_store[p], 16)
            if p == 1:
                sp.wait_ge(s_vals, 2 * (n + 1))
                vd = v_heads.rearrange("b h p c w -> b p h (c w)")
                sp.dma_start(vd[m // 4, :, :, bass.ds((m % 4) * 8 * VW, 8 * VW)],
                             vals[:, r // 2 % 2].rearrange("p h c w -> p h (c w)")).then_inc(s_vstore[r // 2 % 2], 16)

        @block.sync
        def _(sp):
            queries["load"](sp)
            for k, name in enumerate(("xk", "xv")):
                sp.dma_start(w_a[:, k, :], a[name + "_w"][0:P]).then_inc(s_w, 16)
                for half in range(2):
                    sp.dma_start(w_b[half * R2:half * R2 + R2, k, :], a[name + "_w"][P:DC]).then_inc(s_w, 16)
                    sp.dma_start(bias[R2 + half:R2 + half + 1, k, :], a[name + "_b"]).then_inc(s_w, 16)
                load(sp, 0, k)
            load(sp, 0, 2)
            load(sp, 0, 3)
            queries["store"](sp)
            with sp.Fori(0, NBLK // 4 - 1) as i:
                for r in range(4):
                    sp.wait_ge(s_v, 2 * (4 * i + r) + 1)
                    load(sp, i + 1, r)
                    store(sp, i, r)
            for r in range(4):
                store(sp, NBLK // 4 - 1, r)
            sp.wait_ge(s_qstore, 16 * 3 * FC)
            for p in range(2):
                sp.wait_ge(s_store[p], 32 * (NBLK // 2))
                sp.wait_ge(s_vstore[p], 16 * (NBLK // 4))

        @block.gpsimd
        def _(g):
            g.memset(ones[R2:R2 + 2, :, :], 1.0).then_inc(s_ones, 1)
            g.wait_ge(s_ones, 1)
            g.memset(vals[:], 1.0).then_inc(s_ones, 1)
            g.wait_ge(s_ones, 2)
            queries["constants_and_norm"](g)

            def work(i, r):
                n, p = 4 * i + r, r % 2
                g.wait_ge(s_lead, 4 * n + 1)
                wait(g, s_v, 2 * (n - 1))
                wait(g, s_lo, n)
                g.tensor_tensor(x_lo[:, p], ctx_a[:, r], x_hi[:, p].bitcast(F32), ALU.subtract).then_inc(s_lo, 1)

            each_block(g, work)

        @block.tensor
        def _(pe):
            queries["products"](pe)
            pe.wait_ge(s_qfull, 4)
            pe.wait_ge(s_wp, 4)
            terms = ((w_hi, x_hi), (w_hi, x_lo), (w_lo, x_hi), (w_both, x_both), (w_last, x_last))

            def work(i, r):
                n, p = 4 * i + r, r % 2
                pe.wait_ge(s_lead, 4 * (n + 1))
                pe.wait_ge(s_lo, n + 1)
                for c in range(FC):
                    wait(pe, s_rest, 2 * (n - 2) + c + 1)
                    for k, (w, x) in enumerate(terms):
                        mm = pe.matmul(psum[:, 2 * p + c, :], w[:, 0, c * P:c * P + P], x[:, p, :],
                                       start=(k == 0), stop=(k == len(terms) - 1))
                    mm.then_inc(s_k, 1)
                for m in range(2):
                    wait(pe, s_vals, 2 * (n - 2) + m + 1)
                    for half in range(2):
                        rows = slice((2 * m + half) * P, (2 * m + half) * P + P)
                        for k, (w, x) in enumerate(terms):
                            mm = pe.matmul(psum[:, 4 + 2 * p + m, half * D:half * D + D], x[:, p, rows],
                                           w[:, 1, :], start=(k == 0), stop=(k == len(terms) - 1))
                    mm.then_inc(s_v, 1)

            each_block(pe, work)

        @block.scalar
        def _(act):
            queries["high_and_middle"](act)
            act.wait_ge(s_ones, 2)

            def work(i, r):
                n, p = 4 * i + r, r % 2
                wait(act, s_store[p], 32 * (2 * i + r // 2))
                for c in range(FC):
                    act.wait_ge(s_k, 2 * n + c + 1)
                    act.copy(parts[:, p, 0, c, :], psum[:, 2 * p + c, :]).then_inc(s_hi, 1)
                for c in range(FC):
                    act.wait_ge(s_rest, 2 * n + c + 1)
                    act.copy(parts[:, p, 1, c, :], rest[:, p, c, :]).then_inc(s_mid, 1)
                for m in range(2):
                    act.wait_ge(s_v, 2 * n + m + 1)
                    if p == 0 and m == 0:
                        wait(act, s_vstore[r // 2], 16 * i)
                    c = 4 * p + 2 * m
                    act.copy(vals[:, r // 2, :, c:c + 2, 0:DH],
                             psum[:, 4 + 2 * p + m, :].rearrange("p (c h d) -> p h c d", c=2, h=H)).then_inc(s_vals, 1)

            each_block(act, work)

        @block.vector
        def _(v):
            queries["norm"](v)
            v.wait_ge(s_w, 16 * 10)
            last = slice(R2, R2 + 2)
            v.tensor_copy(w_hi[:], w_a[:]).then_inc(s_wh, 1)
            v.tensor_copy(w_both[:], w_b[:]).then_inc(s_wh, 1)
            v.tensor_copy(bias_hi[last], bias[last]).then_inc(s_wh, 1)
            v.wait_ge(s_wh, 3)
            v.tensor_tensor(w_lo[:], w_a[:], w_hi[:].bitcast(F32), ALU.subtract).then_inc(s_wp, 1)
            v.tensor_tensor(w_last[0:R2], w_b[0:R2], w_both[0:R2].bitcast(F32), ALU.subtract).then_inc(s_wp, 1)
            v.tensor_tensor(w_last[last], bias[last], bias_hi[last].bitcast(F32), ALU.subtract).then_inc(s_wh, 1)
            v.wait_ge(s_wh, 4)
            v.tensor_copy(w_last[R2:R2 + 1], bias[R2:R2 + 1]).then_inc(s_wp, 1)
            v.wait_ge(s_ones, 1)
            v.tensor_copy(x_last[last], ones[last]).then_inc(s_wp, 1)

            def lead(i, r):
                n, p = 4 * i + r, r % 2
                v.wait_ge(s_ctx[r % 4], 32 * (i + r // 4 + 1))
                wait(v, s_v, 2 * (n - 1))
                v.tensor_copy(x_hi[:, p], ctx_a[:, r % 4]).then_inc(s_lead, 1)
                v.tensor_copy(x_both[0:R2, p], ctx_b[:, r % 4]).then_inc(s_lead, 1)
                v.tensor_copy(x_last[0:R2, p], ctx_b[:, r % 4]).then_inc(s_lead, 1)
                v.wait_ge(s_lead, 4 * n + 3)
                v.tensor_tensor(x_both[R2:, p], ctx_b[:, r % 4], x_last[0:R2, p].bitcast(F32),
                                ALU.subtract).then_inc(s_lead, 1)

            def work(i, r, end=False):
                n, p = 4 * i + r, r % 2
                if not end:
                    lead(i, r + 1)
                for c in range(FC):
                    v.wait_ge(s_hi, 2 * n + c + 1)
                    wait(v, s_mid, 2 * (n - 2) + c + 1)
                    wait(v, s_low, 2 * (n - 2) + c + 1)
                    v.tensor_tensor(rest[:, p, c, :], psum[:, 2 * p + c, :], parts[:, p, 0, c, :],
                                    ALU.subtract).then_inc(s_rest, 1)
                for c in range(FC):
                    v.wait_ge(s_mid, 2 * n + c + 1)
                    v.tensor_tensor(parts[:, p, 2, c, :], rest[:, p, c, :], parts[:, p, 1, c, :],
                                    ALU.subtract).then_inc(s_low, 1)

            lead(0, 0)
            queries["full"](v)
            queries["rest_and_low"](v)
            for r in range(4):
                work(0, r)
            with v.Fori(1, NBLK // 4 - 1) as i:
                for r in range(4):
                    work(i, r)
            for r in range(4):
                work(NBLK // 4 - 1, r, end=(r == 3))


def cross_attention(nc, a, psum, identb, k_parts, q_parts, v_heads, o_all, wo, bo, s_wo):
    BUFS = 4
    with ExitStack() as life:
        def sb(name, shape, dt):
            return life.enter_context(nc.sbuf_tensor(name, shape, dt))

        def sem(name):
            return life.enter_context(nc.semaphore(name))

        ROWS = PARTS + 4
        k_st = [sb(f"k_st{n}", [ROWS, S], BF16) for n in range(BUFS)]
        q_st = [sb(f"q_st{n}", [ROWS, T], BF16) for n in range(BUFS)]
        v_st = [sb(f"v_st{n}", [P, NC * VW], F32) for n in range(BUFS)]
        probs = sb("probs", [P, 2, NC * T], F32)
        mx = sb("mx", [P, 2, 8], F32)
        raw_m = sb("raw_m", [P, 2], F32)
        neg_m = sb("neg_m", [P, 2], F32)
        m_rest = sb("m_rest", [P, 2], F32)
        m_parts = sb("m_parts", [P, 2, 4], BF16)
        flag = sb("flag", [P, 2], mybir.dt.int32)
        pv_sb = sb("pv_sb", [P, T], F32)
        pick = sb("pick", [P, VW], F32)
        recip = sb("recip", [P, 2], F32)
        spare = sb("spare", [1, 4], F32)
        s_kq = [sem(f"xa_kq{n}") for n in range(BUFS)]
        s_vl = [sem(f"xa_vl{n}") for n in range(BUFS)]
        names = ("const", "pick", "m_ready", "m_read", "raw", "neg", "high", "rest", "mid", "parts", "turned", "row",
                 "flag", "s_ready", "exp", "clamp", "fixed", "parts0", "pv", "pv_read", "o", "o_div", "o_read")
        s = {n: sem("xa_" + n) for n in names}
        S_BANK, M_BANK, PV_BANK, MISC = 0, 2, 6, 7
        block = life.enter_context(nc.Block())

        def head(i, r):
            h = BUFS * i + r
            return h if not isinstance(h, int) or 0 <= h < NH else None

        def periods(engine, slot):
            def period(i, r):
                for jj in range(8):
                    slot(i, r, jj)
            for r in range(-1, 3):
                period(0, r)
            with engine.Fori(0, NH // BUFS - 1) as i:
                for r in range(3, 3 + BUFS):
                    period(i, r)
            for r in range(3, 6):
                period(NH // BUFS - 1, r)

        def stages(i, r, jj):
            return (i, r + 1, jj), (i, r - (jj < 3), (jj - 3) % 8), (i, r - 1 - (jj < 5), (jj - 5) % 8)

        @block.sync
        def _(sp):
            sp.dma_start(pick[:], a["pick"]).then_inc(s["pick"], 16)

            def load(i, b):
                h = BUFS * i + b
                wait(sp, s["s_ready"], 16 * (h - BUFS + 1))
                for m in range(3):
                    first, count = (0, 3, 5)[m], 3 - m
                    rows = slice(first * DH, (first + count) * DH)
                    sp.dma_start(k_st[b][rows, :], k_parts[m:m + 1, h].broadcast_to([count, DH, S])).then_inc(s_kq[b], 16)
                    sp.dma_start(q_st[b][rows, :], q_parts[0:count, h]).then_inc(s_kq[b], 16)
                wait(sp, s["pv"], 8 * (h - BUFS + 1))
                sp.dma_start(v_st[b][:], v_heads.rearrange("b h p c w -> (b h) p (c w)")[h]).then_inc(s_vl[b], 16)

            for b in range(BUFS):
                load(0, b)
            for k, name in enumerate(("xo_w", "so_w")):
                sp.dma_start(wo[:, k], a[name].rearrange("(c p) n -> p c n", p=P)).then_inc(s_wo, 16)
            sp.dma_start(bo[:], a["xo_b"]).then_inc(s_wo, 16)
            with sp.Fori(1, NH // BUFS) as i:
                for b in range(BUFS):
                    load(i, b)

        @block.gpsimd
        def _(g):
            for n in range(1, BUFS):
                g.memset(k_st[n][PARTS:ROWS, :], 1.0).then_inc(s["const"], 1)
                g.wait_ge(s["const"], 2 * n - 1)
                g.memset(k_st[n][PARTS:PARTS + 1, :], 0.0).then_inc(s["const"], 1)

        @block.tensor
        def _(pe):
            def maxima(i, r, jj):
                h, b = head(i, r), r % BUFS
                if h is None:
                    return
                if jj == 0:
                    pe.wait_ge(s_kq[b], 16 * 6 * (i + r // BUFS + 1))
                wait(pe, s["m_read"], 8 * h + jj - 1)
                qc, kb = jj // 4, 2 * (jj % 4)
                for k in range(2):
                    mm = pe.matmul(psum[:, M_BANK + 2 * (jj % 2) + k, :], q_st[b][0:PARTS, qc * P:qc * P + P],
                                   k_st[b][0:PARTS, (kb + k) * 512:(kb + k + 1) * 512], start=True, stop=True)
                mm.then_inc(s["m_ready"], 1)

            def scores(i, r, jj, odd):
                h, b = head(i, r), r % BUFS
                if h is None:
                    return
                j = 2 * jj + odd
                if j == 0:
                    pe.wait_ge(s["row"], h + 1)
                    pe.wait_ge(*((s["const"], 2 * b) if b else (s["fixed"], 3)))
                wait(pe, s["exp"], 16 * h + j - 1)
                for k in range(2):
                    c = 2 * j + k
                    mm = pe.matmul(psum[:, S_BANK + j % 2, k * T:k * T + T], k_st[b][:, c * P:c * P + P],
                                   q_st[b][:, :], start=True, stop=True)
                mm.then_inc(s["s_ready"], 1)

            def values(i, r, jj):
                h, b = head(i, r), r % BUFS
                if h is None:
                    return
                if jj == 0:
                    pe.wait_ge(s["clamp"], h + 1)
                    pe.wait_ge(s_vl[b], 16 * (i + r // BUFS + 1))
                    pe.wait_ge(s["fixed"], 1)
                    wait(pe, s["pv_read"], h)
                for g in range(4):
                    c = 4 * jj + g
                    mm = pe.matmul(psum[32 * g:32 * g + VW, PV_BANK, 0:T], v_st[b][:, c * VW:c * VW + VW],
                                   probs[:, r % 2, c * T:c * T + T], start=(jj == 0), stop=(jj == 7))
                mm.then_inc(s["pv"], 1)

            def turn_maxima(i, r):
                h = head(i, r)
                if h is None:
                    return
                pe.wait_ge(s["parts"], h + 1)
                wait(pe, s["o_read"], h - 2)
                for qc in range(2):
                    mm = pe.matmul(psum[96:100, MISC, qc * P:qc * P + P], m_parts[:, qc, :], identb[:],
                                   start=True, stop=True)
                mm.then_inc(s["turned"], 1)

            def output(i, r):
                h = head(i, r)
                if h is None:
                    return
                pe.wait_ge(s["pv_read"], h + 1)
                wait(pe, s["o_read"], h)
                pe.wait_ge(s["row"], NH if isinstance(h, int) and h > NH - 3 else h + 3)
                for qc in range(2):
                    mm = pe.matmul(psum[:, MISC, 256 + qc * VW:256 + qc * VW + VW], pv_sb[:, qc * P:qc * P + P],
                                   pick[:], start=True, stop=True)
                mm.then_inc(s["o"], 1)

            def slot(i, r, jj):
                of_max, of_scores, of_values = stages(i, r, jj)
                maxima(*of_max)
                if jj == 6:
                    output(i, r - 2)
                scores(*of_scores, 0)
                if jj == 2:
                    turn_maxima(i, r)
                values(*of_values)
                scores(*of_scores, 1)

            pe.wait_ge(s["pick"], 16)
            periods(pe, slot)

        @block.scalar
        def _(act):
            def exps(i, r, jj, odd):
                h = head(i, r)
                if h is None:
                    return
                j = 2 * jj + odd
                act.wait_ge(s["s_ready"], 16 * h + j + 1)
                if not odd:
                    wait(act, s["pv"], 8 * (h - 2) + jj + 1)
                act.activation(probs[:, r % 2, j * 512:j * 512 + 512], psum[:, S_BANK + j % 2, :],
                               ACT.Exp).then_inc(s["exp"], 1)

            def slot(i, r, jj):
                _, of_scores, _ = stages(i, r, jj)
                exps(*of_scores, 0)
                h = head(i, r - 2)
                if jj == 4 and h is not None:
                    act.wait_ge(s["pv"], 8 * (h + 1))
                    wait(act, s["o"], h)
                    act.copy(pv_sb[:], psum[:, PV_BANK, 0:T]).then_inc(s["pv_read"], 1)
                h = head(i, r)
                if jj == 2 and h is not None:
                    act.wait_ge(s["turned"], h + 1)
                    wait(act, s["s_ready"], 16 * (h - 3))
                    act.copy(q_st[r % BUFS][PARTS:PARTS + 4, :], psum[96:100, MISC, 0:T]).then_inc(s["row"], 1)
                exps(*of_scores, 1)

            periods(act, slot)

        @block.vector
        def _(v):
            v.memset(psum[:, PV_BANK, 0:T], 0.0).then_inc(s["fixed"], 1)
            v.memset(k_st[0][PARTS:ROWS, :], 1.0).then_inc(s["fixed"], 1)
            v.wait_ge(s["fixed"], 2)
            v.memset(k_st[0][PARTS:PARTS + 1, :], 0.0).then_inc(s["fixed"], 1)
            flag_reg = life.enter_context(v.register("clip_flag"))

            def row_max(i, r, jj):
                h = head(i, r)
                if h is None:
                    return
                v.wait_ge(s["m_ready"], 8 * h + jj + 1)
                v.tensor_reduce(mx[:, r % 2, jj:jj + 1], psum[:, M_BANK + 2 * (jj % 2):M_BANK + 2 * (jj % 2) + 2, :],
                                AX.XY, ALU.max).then_inc(s["m_read"], 1)

            def chain(i, r, step):
                h = head(i, r)
                if h is None:
                    return
                inside, hi, mid, low = (m_parts[:, :, k] for k in range(4))
                if step == 0:
                    v.wait_ge(s["m_read"], 8 * h + 8)
                    v.tensor_reduce(raw_m[:], mx[:, r % 2, :].rearrange("p (q k) -> p q k", q=2), AX.X, ALU.max,
                                    negate=True).then_inc(s["raw"], 1)
                elif step == 1:
                    v.wait_ge(s["raw"], h + 1)
                    wait(v, s["turned"], h)
                    v.tensor_scalar(neg_m[:], raw_m[:], CLAMP - LOW, -CLAMP, ALU.min, ALU.max).then_inc(s["neg"], 1)
                    v.tensor_scalar(hi, raw_m[:], CLAMP - LOW, -CLAMP, ALU.min, ALU.max).then_inc(s["high"], 1)
                elif step == 2:
                    v.wait_ge(s["neg"], h + 1)
                    v.wait_ge(s["high"], h + 1)
                    v.tensor_tensor(m_rest[:], neg_m[:], hi, ALU.subtract).then_inc(s["rest"], 1)
                    v.tensor_tensor(inside, raw_m[:], neg_m[:], ALU.not_equal).then_inc(s["parts0"], 1)
                elif step == 3:
                    v.wait_ge(s["rest"], h + 1)
                    v.tensor_copy(mid, m_rest[:]).then_inc(s["mid"], 1)
                else:
                    v.wait_ge(s["mid"], h + 1)
                    v.wait_ge(s["parts0"], h + 1)
                    v.tensor_tensor(low, m_rest[:], mid, ALU.subtract).then_inc(s["parts"], 1)

            def read_flag(i, r):
                h = head(i, r)
                if h is None:
                    return
                v.wait_ge(s["row"], h + 1)
                v.tensor_reduce(flag[96:97, r % 2:r % 2 + 1], q_st[r % BUFS][96:97, :], AX.X, ALU.max).then_inc(s["flag"], 1)

            def clamp(i, r):
                h = head(i, r)
                if h is None:
                    return
                v.wait_ge(s["exp"], 16 * (h + 1))
                v.wait_ge(s["flag"], h + 1)
                v.memset(spare[:, r % 2:r % 2 + 1], 0.0)
                v.reg_load(flag_reg, flag[96:97, r % 2:r % 2 + 1])
                with v.If_ne(flag_reg, 0):
                    p = probs[:, r % 2, :]
                    v.tensor_scalar(p, p, 1.0, FLOOR, ALU.min, ALU.max).then_inc(s["clamp"], 1)
                with v.Else():
                    v.memset(spare[:, 2 + r % 2:3 + r % 2], 0.0).then_inc(s["clamp"], 1)

            def finish(i, r):
                h = head(i, r)
                if h is None:
                    return
                v.wait_ge(s["o"], h + 1)
                wait(v, s["o_read"], h)
                o = psum[:, MISC, 256:256 + 2 * VW].rearrange("p (q w) -> p q w", q=2)
                v.reciprocal(recip[:], o[:, :, DH]).then_inc(s["o_div"], 1)
                v.wait_ge(s["o_div"], h + 1)
                v.tensor_tensor(o_all[:, :, bass.ds(h * DH, DH)], o[:, :, 0:DH],
                                recip[:].unsqueeze(2).broadcast_to([P, 2, DH]), ALU.mult).then_inc(s["o_read"], 1)

            def slot(i, r, jj):
                of_max, _, _ = stages(i, r, jj)
                if jj == 0:
                    chain(i, r, 0)
                    chain(i, r, 1)
                row_max(*of_max)
                if jj == 0:
                    chain(i, r, 2)
                    chain(i, r, 3)
                    chain(i, r, 4)
                if jj == 3:
                    read_flag(i, r)
                    clamp(i, r - 1)
                if jj == 7:
                    finish(i, r - 2)

            periods(v, slot)


def attention_output(nc, which, w, b, s_weights, weights, psum, x_sb, ident, ones_row, o_all, oT, neg_half, stats, mv, ve,
                     rstd):
    with ExitStack() as life:
        def sem(name):
            return life.enter_context(nc.semaphore(name))

        s_turn, s_oT, s_y, s_x, s_stat, s_rstd = (
            sem(which + n) for n in ("_turn", "_oT", "_y", "_x", "_stat", "_rstd"))
        block = life.enter_context(nc.Block())

        @block.gpsimd
        def _(g):
            row_scales(g, ve, neg_half, rstd, s_stat, s_rstd)

        @block.tensor
        def _(pe):
            for n in range(4):
                for k in range(4):
                    t = 4 * (n % 2) + k
                    src = o_all[:, t % 2, (t // 2) * D + (n // 2) * P:(t // 2) * D + (n // 2) * P + P]
                    mm = pe.transpose(psum[:, n, k * P:k * P + P], src, ident[:])
                mm.then_inc(s_turn, 1)
            pe.wait_ge(s_weights, 16 * weights)
            pe.wait_ge(s_oT, 4)
            for t in range(NT):
                bank = psum[:, 4 + t // 2, (t % 2) * D:(t % 2) * D + D]
                for c in range(FC):
                    mm = pe.matmul(bank, oT[:, c, t * P:t * P + P], w[:, c, :], start=(c == 0),
                                   stop=(b is None and c == FC - 1))
                if b is not None:
                    mm = pe.matmul(bank, ones_row[:], b[:], start=False, stop=True)
                if t % 2:
                    mm.then_inc(s_y, 1)

        @block.vector
        def _(v):
            for n in range(4):
                v.wait_ge(s_turn, n + 1)
                v.tensor_copy(oT[:, n // 2, (n % 2) * 512:(n % 2) * 512 + 512], psum[:, n, :]).then_inc(s_oT, 1)
            for m in range(NT // 2):
                v.wait_ge(s_y, m + 1)
                v.tensor_tensor(x_sb[:, 2 * m:2 * m + 2, :], x_sb[:, 2 * m:2 * m + 2, :],
                                psum[:, 4 + m, :].rearrange("p (t d) -> p t d", t=2), ALU.add).then_inc(s_x, 1)
                v.wait_ge(s_x, m + 1)
                tile_statistics(v, x_sb, stats, (2 * m, 2 * m + 1), s_stat)
            row_variances(v, stats, mv, ve, s_stat)


def self_attention(nc, a, psum, x_sb, ident, identb, mv, rstd, xn, xnT, qk_stacked, o_all):
    with ExitStack() as outer:
        v_all = outer.enter_context(nc.sbuf_tensor("v_all", [P, NT, H * VW], F32))
        with ExitStack() as life:
            def sb(name, shape, dt):
                return life.enter_context(nc.sbuf_tensor(name, shape, dt))

            def sem(name):
                return life.enter_context(nc.semaphore(name))

            w = sb("w_qkv", [P, 5, FC, D], F32)
            cos = sb("cos", [P, 512], F32)
            sin = sb("sin", [P, 512], F32)
            direct = sb("direct", [P, 8, 512], F32)
            swapped = sb("swapped", [P, 8, 512], F32)
            parts = sb("qk_bf", [P, 3, 8, 512], BF16)
            s_load, s_turned, s_mm, s_read, s_add, s_vmm, s_v, s_store = (
                sem(n) for n in ("sp_load", "sp_turned", "sp_mm", "sp_read", "sp_add", "sp_vmm", "sp_v", "sp_store"))
            s_hi, s_rest, s_mid, s_low, s_one = (sem(n) for n in ("sp_hi", "sp_rest", "sp_mid", "sp_low", "sp_one"))
            block = life.enter_context(nc.Block())
            norm_dve, norm_pe = norm_and_turn("ln2", psum, x_sb, ident, mv, rstd, xn, xnT, s_turned, sem)

            @block.sync
            def _(sp):
                for n, name in enumerate(("sq_w", "sk_w", "sq_sw", "sk_sw", "sv_w")):
                    sp.dma_start(w[:, n], a[name].rearrange("(c p) n -> p c n", p=P)).then_inc(s_load, 16)
                sp.dma_start(cos[:], a["cos"]).then_inc(s_load, 16)
                sp.dma_start(sin[:], a["sin"]).then_inc(s_load, 16)
                for n in range(2 * FC):
                    kind, c = n // FC, n % FC
                    sp.wait_ge(s_low, 2 * n + 2)
                    for g in range(6):
                        part = (Q_PART, K_PART)[kind][g]
                        sp.dma_start(qk_stacked[kind, c * (H // FC):(c + 1) * (H // FC), g * DH:g * DH + DH, :],
                                     parts[:, part, 2 * n:2 * n + 2, :].rearrange("p m t -> p (m t)")
                                     ).then_inc(s_store, 16)
                sp.wait_ge(s_store, 16 * 6 * 2 * FC)

            @block.gpsimd
            def _(g):
                g.memset(v_all[:], 1.0).then_inc(s_one, 1)
                g.wait_ge(s_one, 1)
                for n in range(8):
                    g.wait_ge(s_hi, n + 1)
                    wait(g, s_rest, n)
                    g.tensor_tensor(swapped[:, n, :], direct[:, n, :], parts[:, 0, n, :], ALU.subtract).then_inc(s_rest, 1)

            @block.tensor
            def _(pe):
                norm_pe(pe)
                pe.wait_ge(s_turned, 4)
                pe.wait_ge(s_load, 16 * 7)
                for n in range(8):
                    kind, fo, half = n // 4, (n // 2) % 2, n % 2
                    if n >= 4:
                        pe.wait_ge(s_read, 2 * (n - 4) + 2)
                    for sw in range(2):
                        for c in range(FC):
                            mm = pe.matmul(psum[:, 2 * (n % 4) + sw, :], w[:, 2 * sw + kind, c, fo * P:fo * P + P],
                                           xnT[:, c, half * 512:half * 512 + 512], start=(c == 0), stop=(c == FC - 1))
                    mm.then_inc(s_mm, 1)
                for t in range(NT):
                    if t % 2 == 0:
                        pe.wait_ge(s_read, 2 * (4 + t // 2) + 2)
                    for c in range(FC):
                        mm = pe.matmul(psum[:, t, 0:D], xnT[:, c, t * P:t * P + P], w[:, 4, c, :], start=(c == 0),
                                       stop=(c == FC - 1))
                    mm.then_inc(s_vmm, 1)

            @block.scalar
            def _(act):
                def middle(n):
                    act.wait_ge(s_rest, n + 1)
                    act.copy(parts[:, 1, n, :], swapped[:, n, :]).then_inc(s_mid, 1)

                for n in range(8):
                    act.wait_ge(s_add, n + 1)
                    act.copy(parts[:, 0, n, :], direct[:, n, :]).then_inc(s_hi, 1)
                    if n:
                        middle(n - 1)
                middle(7)
                act.wait_ge(s_one, 1)
                for t in range(NT):
                    act.wait_ge(s_vmm, t + 1)
                    act.copy(v_all[:, t, :].rearrange("p (h w) -> p h w", h=H)[:, :, 0:DH],
                             psum[:, t, 0:D].rearrange("p (h d) -> p h d", h=H)).then_inc(s_v, 1)

            @block.vector
            def _(v):
                def low(n):
                    v.wait_ge(s_mid, n + 1)
                    v.tensor_tensor(parts[:, 2, n, :], swapped[:, n, :], parts[:, 1, n, :], ALU.subtract).then_inc(s_low, 1)

                norm_dve(v)
                v.wait_ge(s_load, 16 * 7)
                for n in range(8):
                    v.wait_ge(s_mm, n + 1)
                    v.tensor_tensor(direct[:, n, :], psum[:, 2 * (n % 4), :], cos[:], ALU.mult).then_inc(s_read, 1)
                    v.tensor_tensor(swapped[:, n, :], psum[:, 2 * (n % 4) + 1, :], sin[:], ALU.mult).then_inc(s_read, 1)
                    v.wait_ge(s_read, 2 * n + 2)
                    v.tensor_tensor(direct[:, n, :], direct[:, n, :], swapped[:, n, :], ALU.add).then_inc(s_add, 1)
                    if n > 1:
                        low(n - 2)
                low(6)
                low(7)

        with ExitStack() as life:
            def sb(name, shape, dt):
                return life.enter_context(nc.sbuf_tensor(name, shape, dt))

            def sem(name):
                return life.enter_context(nc.semaphore(name))

            G, SLOTS = 4, 4
            GROUPS, BLK = NH // G, 3 * P
            ROWS = PARTS + 3
            q_st = [sb(f"sq_st{s}", [ROWS, G * T], BF16) for s in range(SLOTS)]
            k_st = [sb(f"sk_st{s}", [ROWS, G * T], BF16) for s in range(SLOTS)]
            vh = [sb(f"svh{s}", [P, 2, G * VW], F32) for s in range(SLOTS)]
            mask = sb("mask", [P, P], F32)
            maskb = sb("maskb", [P, P], BF16)
            probs = sb("sprobs", [P, 2, G, BLK], F32)
            mx = sb("smx", [P, 2, G, 3], F32)
            raw_m = sb("sraw_m", [P, G, 2], F32)
            neg_m = sb("sneg_m", [P, G, 2], F32)
            m_rest = sb("sm_rest", [P, G, 2], F32)
            m_parts = sb("sm_parts", [P, G, 2, 4], BF16)
            pv_sb = sb("spv_sb", [P, T], F32)
            recip = sb("srecip", [P, 2, G], F32)
            s_qk = [sem(f"sa_qk{s}") for s in range(SLOTS)]
            s_vl = [sem(f"sa_vl{s}") for s in range(SLOTS)]
            s_mask = sem("sa_mask")
            names = ("const", "m_ready", "m_read", "raw", "neg", "high", "rest", "mid", "parts", "turned", "row", "s_ready",
                     "exp", "pv", "pv_read", "o", "o_div", "o_read")
            s = {n: sem("sa_" + n) for n in names}
            M_BANK, S_BANK, TURN, PV_BANK, O_BANK = 0, 2, 4, 6, 7
            block = life.enter_context(nc.Block())

            def periods(engine, step):
                for r in range(SLOTS):
                    step(0, r)
                with engine.Fori(1, GROUPS // SLOTS) as i:
                    for r in range(SLOTS):
                        step(i, r)
                for r in range(4):
                    step(GROUPS // SLOTS, r)

            def group(i, r):
                n = SLOTS * i + r
                return n if not isinstance(n, int) or 0 <= n < GROUPS else None

            @block.sync
            def _(sp):
                sp.dma_start(mask[:], a["mask"]).then_inc(s_mask, 16)

                def load(i, slot):
                    n = SLOTS * i + slot
                    wait(sp, s["s_ready"], G * (n - SLOTS + 1))
                    for kind, dst in enumerate((q_st, k_st)):
                        src = qk_stacked[kind, slot * G:slot * G + G, :, bass.ds(i * T, T)].rearrange("h r t -> r h t")
                        sp.dma_start(dst[slot][0:PARTS, :].rearrange("r (h t) -> r h t", h=G), src
                                     ).then_inc(s_qk[slot], 16)
                    wait(sp, s["pv"], n - SLOTS + 1)
                    sp.dma_start(vh[slot][:], v_all[:, bass.ds(i * 2, 2), slot * G * VW:(slot + 1) * G * VW]
                                 ).then_inc(s_vl[slot], 16)

                for slot in range(SLOTS):
                    load(0, slot)
                with sp.Fori(1, GROUPS // SLOTS) as i:
                    for slot in range(SLOTS):
                        load(i, slot)

            @block.gpsimd
            def _(g):
                for slot in range(SLOTS):
                    g.memset(k_st[slot][PARTS:ROWS, :], 1.0).then_inc(s["const"], 1)

            @block.tensor
            def _(pe):
                def maxima(i, r, j):
                    n = group(i, r)
                    if n is None:
                        return
                    slot = r % SLOTS
                    if j == 0:
                        pe.wait_ge(s_qk[slot], 32 * (i + r // SLOTS + 1))
                    wait(pe, s["m_read"], G * n + j - 1)
                    bank = psum[:, M_BANK + j % 2, :]
                    q, k = q_st[slot][0:PARTS, j * T:j * T + T], k_st[slot][0:PARTS, j * T:j * T + T]
                    pe.matmul(bank[:, 0:P], q[:, 0:P], k[:, 0:P], start=True, stop=False)
                    pe.matmul(bank[:, 0:P], identb[:], maskb[:], start=False, stop=True)
                    pe.matmul(bank[:, P:3 * P], q[:, P:T], k, start=True, stop=False)
                    pe.matmul(bank[:, 2 * P:3 * P], identb[:], maskb[:], start=False, stop=True).then_inc(s["m_ready"], 1)

                def turn_maxima(i, r):
                    n = group(i, r)
                    if n is None:
                        return
                    pe.wait_ge(s["parts"], n + 1)
                    wait(pe, s["row"], 2 * n)
                    for j in range(G):
                        for qc in range(2):
                            col = (j % 2) * T + qc * P
                            mm = pe.matmul(psum[PARTS:ROWS, TURN + j // 2, col:col + P], m_parts[:, j, qc, 0:3],
                                           identb[:], start=True, stop=True)
                    mm.then_inc(s["turned"], 1)

                def scores(i, r, j):
                    n = group(i, r)
                    if n is None:
                        return
                    slot = r % SLOTS
                    if j % 2 == 0:
                        pe.wait_ge(s["row"], 2 * n + j // 2 + 1)
                    if j == 0:
                        pe.wait_ge(s["const"], SLOTS)
                    wait(pe, s["exp"], G * n + j - 1)
                    bank = psum[:, S_BANK + j % 2, :]
                    q, k = q_st[slot][:, j * T:j * T + T], k_st[slot][:, j * T:j * T + T]
                    pe.matmul(bank[:, 0:T], k[:, 0:P], q, start=True, stop=False)
                    pe.matmul(bank[:, 0:P], maskb[:], identb[:], start=False, stop=True)
                    pe.matmul(bank[:, T:T + P], k[:, P:T], q[:, P:T], start=True, stop=False)
                    pe.matmul(bank[:, T:T + P], maskb[:], identb[:], start=False, stop=True).then_inc(s["s_ready"], 1)

                def values(i, r):
                    n = group(i, r)
                    if n is None:
                        return
                    slot, par = r % SLOTS, r % 2
                    pe.wait_ge(s_vl[slot], 16 * (i + r // SLOTS + 1))
                    pe.wait_ge(s["exp"], G * (n + 1))
                    wait(pe, s["pv_read"], n)
                    for kc in range(2):
                        for j in range(G):
                            mm = pe.matmul(psum[32 * j:32 * j + VW, PV_BANK, kc * P:T],
                                           vh[slot][:, kc, j * VW:j * VW + VW],
                                           probs[:, par, j, kc * T:kc * P + T], start=(kc == 0), stop=(kc == 1))
                    mm.then_inc(s["pv"], 1)

                def output(i, r):
                    n = group(i, r)
                    if n is None:
                        return
                    pe.wait_ge(s["pv_read"], n + 1)
                    wait(pe, s["o_read"], n)
                    for qc in range(2):
                        mm = pe.transpose(psum[:, O_BANK, qc * P:qc * P + P], pv_sb[:, qc * P:qc * P + P], ident[:])
                    mm.then_inc(s["o"], 1)

                def step(i, r):
                    for j in range(G):
                        maxima(i, r, j)
                        if j == 1:
                            values(i, r - 3)
                        if j == 3:
                            output(i, r - 3)
                        scores(i, r - 2, j)
                        if j == 1:
                            turn_maxima(i, r - 1)

                pe.wait_ge(s["raw"], 1)
                periods(pe, step)

            @block.scalar
            def _(act):
                def step(i, r):
                    for j in range(G):
                        n = group(i, r - 2)
                        if n is not None:
                            act.wait_ge(s["s_ready"], G * n + j + 1)
                            if j == 0:
                                wait(act, s["pv"], n - 1)
                            act.activation(probs[:, r % 2, j, :], psum[:, S_BANK + j % 2, 0:BLK], ACT.Exp,
                                           scale=SCALE).then_inc(s["exp"], 1)
                        n = group(i, r - 3)
                        if j == 1 and n is not None:
                            act.wait_ge(s["pv"], n + 1)
                            wait(act, s["o"], n)
                            act.copy(pv_sb[:], psum[:, PV_BANK, 0:T]).then_inc(s["pv_read"], 1)
                        n = group(i, r - 1)
                        if j >= 2 and n is not None:
                            act.wait_ge(s["turned"], n + 1)
                            m = j - 2
                            act.copy(q_st[(r - 1) % SLOTS][PARTS:ROWS, 2 * m * T:2 * (m + 1) * T],
                                     psum[PARTS:ROWS, TURN + m, :]).then_inc(s["row"], 1)

                periods(act, step)

            @block.vector
            def _(v):
                v.wait_ge(s_mask, 16)
                v.memset(psum[:, PV_BANK, 0:T], 0.0)
                v.tensor_copy(maskb[:], mask[:]).then_inc(s["raw"], 1)

                def row_max(i, r, j):
                    n = group(i, r)
                    if n is None:
                        return
                    v.wait_ge(s["m_ready"], G * n + j + 1)
                    v.tensor_reduce(mx[:, r % 2, j, :], psum[:, M_BANK + j % 2, 0:BLK].rearrange("p (s k) -> p s k", s=3),
                                    AX.X, ALU.max).then_inc(s["m_read"], 1)

                def chain(i, r, steps):
                    n = group(i, r)
                    if n is None:
                        return
                    hi, mid, low = (m_parts[:, :, :, k] for k in range(3))
                    if 0 in steps:
                        v.wait_ge(s["m_read"], G * (n + 1))
                        v.tensor_tensor(raw_m[:], mx[:, r % 2, :, 0:2], mx[:, r % 2, :, 0:3:2], ALU.max).then_inc(s["raw"], 1)
                        v.wait_ge(s["raw"], n + 2)
                        wait(v, s["turned"], n)
                        v.tensor_scalar(neg_m[:], raw_m[:], -1.0, None, ALU.mult).then_inc(s["neg"], 1)
                        v.tensor_scalar(hi, raw_m[:], -1.0, None, ALU.mult).then_inc(s["high"], 1)
                    if 1 in steps:
                        v.wait_ge(s["neg"], n + 1)
                        v.wait_ge(s["high"], n + 1)
                        v.tensor_tensor(m_rest[:], neg_m[:], hi, ALU.subtract).then_inc(s["rest"], 1)
                        v.wait_ge(s["rest"], n + 1)
                        v.tensor_copy(mid, m_rest[:]).then_inc(s["mid"], 1)
                        v.wait_ge(s["mid"], n + 1)
                        v.tensor_tensor(low, m_rest[:], mid, ALU.subtract).then_inc(s["parts"], 1)

                def finish(i, r):
                    n = group(i, r)
                    if n is None:
                        return
                    v.wait_ge(s["o"], n + 1)
                    o = psum[:, O_BANK, 0:T].rearrange("p (q h w) -> p q h w", q=2, h=G)
                    v.reciprocal(recip[:], o[:, :, :, DH]).then_inc(s["o_div"], 1)
                    v.wait_ge(s["o_div"], n + 1)
                    v.tensor_tensor(o_all[:, :, bass.ds(n * G * DH, G * DH)].rearrange("p q (h d) -> p q h d", h=G),
                                    o[:, :, :, 0:DH], recip[:].unsqueeze(3).broadcast_to([P, 2, G, DH]),
                                    ALU.mult).then_inc(s["o_read"], 1)

                def step(i, r):
                    for j in range(G):
                        if j == 0:
                            chain(i, r - 1, (0,))
                        row_max(i, r, j)
                        if j == 0:
                            chain(i, r - 1, (1,))
                        if j == 1:
                            finish(i, r - 4)

                periods(v, step)


def experts(nc, a, psum, x_sb, ident, ones_row, mv, rstd, xn, xnT, out):
    with ExitStack() as life:
        def sb(name, shape, dt):
            return life.enter_context(nc.sbuf_tensor(name, shape, dt))

        def sem(name):
            return life.enter_context(nc.semaphore(name))

        wr = sb("wr", [P, FC, E], F32)
        br = sb("br", [1, E], F32)
        b1 = sb("b1", [P, E, HC], F32)
        b1_cur = sb("b1_cur", [P, 2, HC], F32)
        b2 = sb("b2", [E, D], F32)
        x_parts = sb("x_parts", [P, 2, FC, TOK], F32R)
        w1 = sb("w1", [P, FC, HID], F32)
        w2 = sb("w2", [P, HC, D], F32)
        w1_parts = sb("w1_parts", [P, 2, FC, HID], F32R)
        w2_parts = sb("w2_parts", [P, 2, HC, D], F32R)
        hid = sb("hid", [P, 4, 512], F32)
        hid_parts = sb("hid_parts", [P, 2, HC, TOK], F32R)
        logits = sb("logits", [P, NT, E], F32)
        top = sb("top", [P, NT, 8], F32)
        shifted = sb("shifted", [P, NT, E], F32)
        gate = sb("gate", [P, NT, E], F32)
        gates = sb("gates", [P, NT, E], F32)
        gsum = sb("gsum", [P, NT], F32)
        grec = sb("grec", [P, NT], F32)
        gatesT = sb("gatesT", [E, TOK], F32)
        gate_cur = sb("gate_cur", [P, 2, NT], F32)
        acc = sb("acc", [P, NT, D], F32)
        s_load, s_turned, s_log, s_g, s_rec, s_gexp, s_gT, s_gTc, s_b2, s_acc0, s_b1, s_gate = (
            sem("ex_" + n) for n in ("load", "turned", "log", "g", "rec", "gexp", "gT", "gTc", "b2", "acc0", "b1", "gate"))
        s_w1, s_w2, s_x1, s_x2, s_w1h, s_w2h, s_w1p, s_w2p, s_hh, s_hp, s_up, s_gelu, s_down, s_acc, s_out = (
            sem("ex_" + n) for n in ("w1", "w2", "x1", "x2", "w1h", "w2h", "w1p", "w2p", "hh", "hp", "up", "gelu", "down",
                                     "acc", "out"))
        GATES_AT, BIAS_AT = 5, 8
        block = life.enter_context(nc.Block())
        norm_dve, norm_pe = norm_and_turn("ln3", psum, x_sb, ident, mv, rstd, xn, xnT, s_turned, sem)

        def each_expert(engine, expert):
            expert(0, 0)
            expert(0, 1)
            with engine.Fori(1, E // 2) as i:
                for p in range(2):
                    expert(i, p)

        @block.sync
        def _(sp):
            sp.dma_start(wr[:], a["r_w"].rearrange("(c p) n -> p c n", p=P)).then_inc(s_load, 16)
            sp.dma_start(br[:], a["r_b"]).then_inc(s_load, 16)
            sp.dma_start(b1[:], a["e1_b"]).then_inc(s_load, 16)
            sp.dma_start(b2[:], a["e2_b"]).then_inc(s_load, 16)

            def expert(i, p):
                e = 2 * i + p
                wait(sp, s_w1p, 2 * e)
                sp.dma_start(w1[:], a["e1_w"][e].rearrange("(c p) n -> p c n", p=P)).then_inc(s_w1, 16)
                wait(sp, s_w2p, 2 * e)
                sp.dma_start(w2[:], a["e2_w"][e].rearrange("(c p) n -> p c n", p=P)).then_inc(s_w2, 16)

            each_expert(sp, expert)
            for half in range(2):
                tiles = slice(half * NT // 2, (half + 1) * NT // 2)
                sp.wait_ge(s_acc, NT * (E - 1) + tiles.stop)
                sp.dma_start(out.rearrange("(t p) d -> p t d", p=P)[:, tiles], acc[:, tiles]).then_inc(s_out, 16)
            sp.wait_ge(s_out, 32)

        @block.tensor
        def _(pe):
            norm_pe(pe)
            pe.wait_ge(s_turned, 4)
            pe.wait_ge(s_load, 64)
            for t in range(NT):
                bank = psum[:, 4, t * E:t * E + E]
                for c in range(FC):
                    pe.matmul(bank, xnT[:, c, t * P:t * P + P], wr[:, c, :], start=(c == 0), stop=False)
                mm = pe.matmul(bank, ones_row[:], br[:], start=False, stop=True)
            mm.then_inc(s_log, 1)
            pe.wait_ge(s_x2, 2)

            def turn_gates():
                pe.wait_ge(s_g, 7)
                for t in range(NT):
                    mm = pe.transpose(psum[0:E, 5 + t // 4, (t % 4) * P:(t % 4) * P + P], gates[:, t, :], ident[:])
                mm.then_inc(s_gT, 1)

            def weigh_biases():
                pe.wait_ge(s_gTc, 1)
                for t in range(NT):
                    mm = pe.matmul(psum[:, 4 + t // 2, (t % 2) * D:(t % 2) * D + D], gatesT[:, t * P:t * P + P], b2[:],
                                   start=True, stop=True)
                mm.then_inc(s_b2, 1)

            def expert(i, p):
                e = 2 * i + p
                first = isinstance(e, int) and e == 0
                pe.wait_ge(s_w1p, 2 * (e + 1))
                for n in range(2 * HC):
                    half, hc = n // HC, n % HC
                    if first and n == GATES_AT:
                        turn_gates()
                    if first and n == BIAS_AT:
                        weigh_biases()
                    wait(pe, s_gelu, 2 * HC * e + n - 3)
                    for k, (wk, xk, c) in enumerate((wk, xk, c) for c in range(FC) for wk, xk in PAIRS):
                        mm = pe.matmul(psum[:, n % 4, :], w1_parts[:, wk, c, hc * P:hc * P + P],
                                       x_parts[:, xk, c, half * 512:half * 512 + 512], start=(k == 0),
                                       stop=(k == 3 * FC - 1))
                    mm.then_inc(s_up, 1)
                pe.wait_ge(s_w2p, 2 * (e + 1))
                if first:
                    pe.wait_ge(s_acc0, 1)
                for t in range(NT):
                    if t % 4 == 0:
                        pe.wait_ge(s_hp, 2 * HC * e + HC * (t // 4 + 1))
                    wait(pe, s_acc, NT * e + t - 3)
                    for k, (hk, wk, c) in enumerate((hk, wk, c) for c in range(HC) for hk, wk in PAIRS):
                        mm = pe.matmul(psum[:, 4 + t % 4, 0:D], hid_parts[:, hk, c, t * P:t * P + P],
                                       w2_parts[:, wk, c, :], start=(k == 0), stop=(k == 3 * HC - 1))
                    mm.then_inc(s_down, 1)

            each_expert(pe, expert)

        @block.scalar
        def _(act):
            act.wait_ge(s_g, 4)
            act.activation(gate[:], shifted[:], ACT.Exp).then_inc(s_gexp, 1)
            act.wait_ge(s_load, 64)

            def expert(i, p):
                e = 2 * i + p
                wait(act, s_gelu, 2 * HC * e)
                act.copy(b1_cur[:, p, :], b1[:, e, :]).then_inc(s_b1, 1)
                act.wait_ge(s_b1, e + 1)
                for n in range(2 * HC):
                    act.wait_ge(s_up, 2 * HC * e + n + 1)
                    wait(act, s_hp, 2 * HC * e + n - 3)
                    act.activation(hid[:, n % 4, :], psum[:, n % 4, :], ACT.Gelu,
                                   bias=b1_cur[:, p, n % HC:n % HC + 1]).then_inc(s_gelu, 1)

            each_expert(act, expert)

        @block.vector
        def _(v):
            norm_dve(v)
            v.wait_ge(s_turned, 4)
            v.tensor_copy(x_parts[:, 0], xnT[:]).then_inc(s_x1, 1)
            v.wait_ge(s_x1, 1)
            v.tensor_tensor(x_parts[:, 1], xnT[:], x_parts[:, 0].bitcast(F32), ALU.subtract).then_inc(s_x2, 2)

            def split_w1(e):
                for c in range(FC):
                    if c == 0:
                        v.wait_ge(s_w1, 16 * (e + 1))
                        wait(v, s_up, 2 * HC * e)
                    v.tensor_copy(w1_parts[:, 0, c], w1[:, c]).then_inc(s_w1h, 1)
                    v.wait_ge(s_w1h, 2 * e + c + 1)
                    v.tensor_tensor(w1_parts[:, 1, c], w1[:, c], w1_parts[:, 0, c].bitcast(F32),
                                    ALU.subtract).then_inc(s_w1p, 1)

            split_w1(0)
            v.wait_ge(s_log, 1)
            v.tensor_copy(logits[:], psum[:, 4, 0:NT * E].rearrange("p (t e) -> p t e", t=NT)).then_inc(s_g, 1)
            v.wait_ge(s_g, 1)
            for t in range(NT):
                last = v.max(top[:, t, :], logits[:, t, :])
            last.then_inc(s_g, 1)
            v.wait_ge(s_g, 2)
            v.tensor_tensor(gates[:], logits[:], top[:, :, 1:2].broadcast_to([P, NT, E]), ALU.is_ge).then_inc(s_g, 1)
            v.tensor_tensor(shifted[:], logits[:], top[:, :, 0:1].broadcast_to([P, NT, E]),
                            ALU.subtract).then_inc(s_g, 1)
            v.wait_ge(s_gexp, 1)
            v.wait_ge(s_g, 4)
            v.tensor_tensor(gate[:], gate[:], gates[:], ALU.mult).then_inc(s_g, 1)
            v.wait_ge(s_g, 5)
            v.tensor_reduce(gsum[:], gate[:], AX.X, ALU.add).then_inc(s_g, 1)
            v.wait_ge(s_g, 6)
            v.reciprocal(grec[:], gsum[:]).then_inc(s_rec, 1)
            v.wait_ge(s_rec, 1)
            v.tensor_tensor(gates[:], gate[:], grec[:].unsqueeze(2).broadcast_to([P, NT, E]), ALU.mult).then_inc(s_g, 1)

            def copy_gates():
                v.wait_ge(s_gT, 1)
                v.tensor_copy(gatesT[:].rearrange("e (a t) -> e a t", a=2), psum[0:E, 5:7, :]).then_inc(s_gTc, 1)

            def start_sum():
                v.wait_ge(s_b2, 1)
                v.tensor_tensor(acc[:], x_sb[:], psum[:, 4:8, :].rearrange("p a (t d) -> p (a t) d", t=2),
                                ALU.add).then_inc(s_acc0, 1)

            def split_w2(e):
                for c in range(2):
                    if c == 0:
                        v.wait_ge(s_w2, 16 * (e + 1))
                        wait(v, s_down, NT * e)
                    rows = slice(4 * c, 4 * c + 4)
                    v.tensor_copy(w2_parts[:, 0, rows], w2[:, rows]).then_inc(s_w2h, 1)
                    v.wait_ge(s_w2h, 2 * e + c + 1)
                    v.tensor_tensor(w2_parts[:, 1, rows], w2[:, rows], w2_parts[:, 0, rows].bitcast(F32),
                                    ALU.subtract).then_inc(s_w2p, 1)

            def lead(e, n):
                half, hc = n // HC, n % HC
                v.wait_ge(s_gelu, 2 * HC * e + n + 1)
                if hc == 0:
                    wait(v, s_down, NT * e - (NT // 2 if half == 0 else 0))
                v.tensor_copy(hid_parts[:, 0, hc, half * 512:half * 512 + 512], hid[:, n % 4, :]).then_inc(s_hh, 1)

            def rest(e, n):
                half, hc = n // HC, n % HC
                v.wait_ge(s_hh, 2 * HC * e + n + 1)
                v.tensor_tensor(hid_parts[:, 1, hc, half * 512:half * 512 + 512], hid[:, n % 4, :],
                                hid_parts[:, 0, hc, half * 512:half * 512 + 512].bitcast(F32),
                                ALU.subtract).then_inc(s_hp, 1)

            def expert(i, p):
                e = 2 * i + p
                first = isinstance(e, int) and e == 0
                if first:
                    v.wait_ge(s_g, 7)
                v.tensor_copy(gate_cur[:, p, :], gates[:, :, bass.ds(e, 1)].rearrange("p t o -> p (t o)")).then_inc(s_gate, 1)
                for n in range(2 * HC):
                    if first and n == GATES_AT:
                        copy_gates()
                    if first and n == BIAS_AT + 1:
                        start_sum()
                    lead(e, n)
                    if n > 0:
                        rest(e, n - 1)
                    if n == 2:
                        split_w2(e)
                rest(e, 2 * HC - 1)
                v.wait_ge(s_gate, e + 1)
                if first:
                    v.wait_ge(s_acc0, 1)
                for t in range(NT):
                    v.wait_ge(s_down, NT * e + t + 1)
                    v.scalar_tensor_tensor(out=acc[:, t, :], in0=psum[:, 4 + t % 4, 0:D], scalar=gate_cur[:, p, t:t + 1],
                                           in1=acc[:, t, :], op0=ALU.mult, op1=ALU.add).then_inc(s_acc, 1)
                    if t == 0 and not (isinstance(e, int) and e == E - 1):
                        split_w1(e + 1)

            expert(0, 0)
            expert(0, 1)
            with v.Fori(1, E // 2 - 1) as i:
                for p in range(2):
                    expert(i, p)
            for p in range(2):
                expert(E // 2 - 1, p)


def constants():
    inv = 1.0 / np.float32(10000.0) ** (np.arange(0, DH, 2, dtype=np.float32) / DH)
    ang = np.arange(T, dtype=np.float32)[:, None] * inv[None, :].astype(np.float32)
    cos = np.concatenate([np.cos(ang), np.cos(ang)], -1).T
    sin = np.concatenate([-np.sin(ang), np.sin(ang)], -1).T
    mask = np.where(np.arange(P)[None, :] > np.arange(P)[:, None], np.float32(-1e30), np.float32(0))
    pick = np.zeros((P, VW), np.float32)
    for g in range(4):
        pick[32 * g + np.arange(VW), np.arange(VW)] = 1.0
    return {
        "ident": np.eye(P, dtype=np.float32), "pick": pick, "mask": mask,
        "cos": np.tile(cos, (P // DH, 2)).astype(np.float32), "sin": np.tile(sin, (P // DH, 2)).astype(np.float32),
    }


def kernel(x, ctx_768, L0_xattn_Wq, L0_xattn_bq, L0_xattn_Wk, L0_xattn_bk, L0_xattn_Wv, L0_xattn_bv, L0_xattn_Wo,
           L0_xattn_bo, L0_attn_Wq, L0_attn_Wk, L0_attn_Wv, L0_attn_Wo, L0_ffn_W1, L0_ffn_b1, L0_ffn_W2, L0_ffn_b2,
           L0_ffn_Wr, L0_ffn_br):
    import concourse.bacc as _bacc
    from concourse.bass_utils import run_bass_kernel_spmd as _run

    def swap(w):
        return np.asarray(w).reshape(H, 2, DH // 2, D)[:, ::-1].reshape(D, D)

    arrays = {
        "x": np.asarray(x).reshape(TOK, D), "ctxT": np.asarray(ctx_768).transpose(0, 2, 1),
        "xq_w": L0_xattn_Wq, "xq_b": np.asarray(L0_xattn_bq).reshape(FC, P).T, "xk_w": L0_xattn_Wk,
        "xk_b": np.asarray(L0_xattn_bk).reshape(1, D), "xv_w": L0_xattn_Wv, "xv_b": np.asarray(L0_xattn_bv).reshape(1, D),
        "xo_w": L0_xattn_Wo, "xo_b": np.asarray(L0_xattn_bo).reshape(1, D),
        "sq_w": np.asarray(L0_attn_Wq).T, "sk_w": np.asarray(L0_attn_Wk).T, "sq_sw": swap(L0_attn_Wq).T,
        "sk_sw": swap(L0_attn_Wk).T, "sv_w": np.asarray(L0_attn_Wv).T, "so_w": np.asarray(L0_attn_Wo).T,
        "r_w": L0_ffn_Wr, "r_b": np.asarray(L0_ffn_br).reshape(1, E), "e1_w": L0_ffn_W1,
        "e1_b": np.asarray(L0_ffn_b1).reshape(E, HC, P).transpose(2, 0, 1), "e2_w": L0_ffn_W2, "e2_b": L0_ffn_b2,
        **constants(),
    }
    arrays = {name: np.ascontiguousarray(v) for name, v in arrays.items()}
    nc = _bacc.Bacc("TRN2", target_bir_lowering=False, num_devices=1)
    args = {name: nc.dram_tensor("in_" + name, v.shape, mybir.dt.from_np(v.dtype), kind="ExternalInput").ap()
            for name, v in arrays.items()}
    out = nc.dram_tensor("out", (TOK, D), F32, kind="ExternalOutput").ap()
    build_program(nc, args, out)
    r = _run(nc, [{"in_" + name: v for name, v in arrays.items()}], core_ids=[0])
    return r.results[0]["out"].reshape(B, T, D)
```
